# Optimizing a Trainium2 kernel written in Bass

```python
import numpy as np
import jax
import jax.numpy as jnp

def _softmax(x, axis=-1):
    return jax.nn.softmax(x, axis=axis)

def _gelu(x):
    return jax.nn.gelu(x, approximate=True)

def _silu(x):
    return jax.nn.silu(x)

def _sigmoid(x):
    return jax.nn.sigmoid(x)

def _layernorm(x, axis=-1, eps=1e-05):
    m = jnp.mean(x, axis=axis, keepdims=True)
    v = jnp.var(x, axis=axis, keepdims=True)
    return (x - m) / jnp.sqrt(v + eps)

def _scatter_add(tgt, idx, src, axis=0):
    return tgt.at[idx].add(src)

def _segment_sum(src, seg, n):
    return jax.ops.segment_sum(src, seg, n)
kernel_name = 'mk_perceiver_d2_seqx_r2_9d626f'

def setup_inputs(seed: int=0):
    np.random.seed(seed)
    _w = jnp.asarray

    def _rec_inputs():
        import jax
        import jax.numpy as jnp
        _rk = jax.random.key(seed)
        x = 7.22e-05 + 1 * jax.random.normal(jax.random.fold_in(_rk, 1), (8, 64, 512), jnp.float32)
        _lenS = 64 - jax.random.randint(jax.random.fold_in(_rk, 7), (8,), 0, max(1, 64 // 4) + 1, jnp.int32)
        _lenS2 = 1601 - jax.random.randint(jax.random.fold_in(_rk, 8), (8,), 0, max(1, 1601 // 4) + 1, jnp.int32)
        _ctx_1024P = jax.random.normal(jax.random.fold_in(_rk, 11), (8, 16, 512), jnp.float32)
        _ctx_1024c = jax.random.dirichlet(jax.random.fold_in(_rk, 511), 0.3 * jnp.ones((16,), jnp.float32), (8, 1601))
        _ctx_1024t = jnp.einsum('bsk,bkd->bsd', _ctx_1024c, _ctx_1024P)
        _ctx_1024t = _ctx_1024t * jax.lax.rsqrt(jnp.mean(jnp.square(_ctx_1024t)) + 1e-12) * 0.953939
        ctx_1024 = 4.13588e-05 + 0.999923 * (_ctx_1024t + 0.3 * jax.random.normal(jax.random.fold_in(_rk, 611), (8, 1601, 512), jnp.float32))
        _validS = jnp.arange(64)[None, :] < _lenS[:, None]
        _validS2 = jnp.arange(1601)[None, :] < _lenS2[:, None]
        _causal = jnp.tril(jnp.ones((64, 64), dtype=bool))
        mask_BxS2_bk0 = jnp.logical_not(jnp.broadcast_to(_validS2[:, :], (8, 1601)))
        return (x, ctx_1024, mask_BxS2_bk0)
    x, ctx_1024, mask_BxS2_bk0 = _rec_inputs()

    def _L0_xattn_setup():
        import jax, jax.numpy as jnp
        import numpy as np
        H = 16
        INPUT_DIM = 512
        FEATURE_DIM = 512
        HEAD_DIM = FEATURE_DIM // H
        key = jax.random.key(seed)
        ks = jax.random.split(key, 12)
        B, S = (4, 1024)
        s = 1.0 / np.sqrt(INPUT_DIM)
        inp = {'data': jax.random.normal(ks[0], (B, S, INPUT_DIM), dtype=jnp.float32), 'context': jax.random.normal(ks[1], (B, S, INPUT_DIM), dtype=jnp.float32), 'wq': jax.random.normal(ks[2], (INPUT_DIM, FEATURE_DIM), dtype=jnp.float32) * s, 'bq': jnp.zeros((FEATURE_DIM,), dtype=jnp.float32), 'wk': jax.random.normal(ks[3], (INPUT_DIM, FEATURE_DIM), dtype=jnp.float32) * s, 'bk': jnp.zeros((FEATURE_DIM,), dtype=jnp.float32), 'wv': jax.random.normal(ks[4], (INPUT_DIM, FEATURE_DIM), dtype=jnp.float32) * s, 'bv': jnp.zeros((FEATURE_DIM,), dtype=jnp.float32), 'wo': jax.random.normal(ks[5], (FEATURE_DIM, INPUT_DIM), dtype=jnp.float32) * s, 'bo': jnp.zeros((INPUT_DIM,), dtype=jnp.float32)}
        return inp
    _L0_xattn_all = _L0_xattn_setup()
    _L0_xattn_in = {k: v for k, v in _L0_xattn_all.items() if k in ('wq', 'bq', 'wk', 'bk', 'wv', 'bv', 'wo', 'bo')}
    del _L0_xattn_all

    def _L0_attn_setup():
        import jax, jax.numpy as jnp
        import numpy as np
        DIM = 512
        NUM_HEADS = 16
        DIM_HEAD = DIM // NUM_HEADS
        NORM = DIM_HEAD ** (-0.5)
        key = jax.random.key(seed)
        k0, k1, k2, k3 = jax.random.split(key, 4)
        B, N = (2, 1024)
        x = jax.random.normal(k0, (B, N, DIM), dtype=jnp.float32)
        Wq = jax.random.normal(k1, (NUM_HEADS, DIM_HEAD, DIM_HEAD), dtype=jnp.float32) * DIM_HEAD ** (-0.5)
        Wp = jax.random.normal(k2, (DIM, DIM), dtype=jnp.float32) * DIM ** (-0.5)
        bp = jax.random.normal(k3, (DIM,), dtype=jnp.float32) * 0.01
        return {'x': x, 'Wq': Wq, 'Wp': Wp, 'bp': bp}
    _L0_attn_all = _L0_attn_setup()
    _L0_attn_in = {k: v for k, v in _L0_attn_all.items() if k in ('Wq', 'Wp', 'bp')}
    del _L0_attn_all

    def _L0_ffn_setup():
        import jax, jax.numpy as jnp
        import numpy as np
        H = 512
        I = 352
        E = 64
        TOP_K = 8
        NG = 8
        TOPK_GROUP = 4
        N_SHARED = 2
        ROUTED_SCALE = 2.5
        S_I = I * N_SHARED

        def _route(x, gate_w, gate_bias):
            T = x.shape[0]
            logits = x @ gate_w.T
            scores = jax.nn.sigmoid(logits)
            scores_for_choice = scores + gate_bias[None, :]
            grp = scores_for_choice.reshape(T, NG, E // NG)
            group_scores = jnp.sum(jax.lax.top_k(grp, 2)[0], axis=-1)
            _, gidx = jax.lax.top_k(group_scores, TOPK_GROUP)
            gmask = jnp.zeros((T, NG), dtype=scores.dtype).at[jnp.arange(T)[:, None], gidx].set(1.0)
            emask = jnp.repeat(gmask, E // NG, axis=1)
            masked = jnp.where(emask > 0, scores_for_choice, 0.0)
            _, topk_idx = jax.lax.top_k(masked, TOP_K)
            topk_w = jnp.take_along_axis(scores, topk_idx, axis=1)
            topk_w = topk_w / (jnp.sum(topk_w, axis=-1, keepdims=True) + 1e-20)
            topk_w = topk_w * ROUTED_SCALE
            rw = jnp.zeros((T, E), dtype=scores.dtype).at[jnp.arange(T)[:, None], topk_idx].add(topk_w)
            return rw

        def _mlp(x, gw, uw, dw):
            return jax.nn.silu(x @ gw.T) * (x @ uw.T) @ dw.T
        key = jax.random.key(seed)
        ks = jax.random.split(key, 10)
        sc = 0.02
        return {'hidden_states': jax.random.normal(ks[0], (1, 512, H), dtype=jnp.float32), 'gate_w': sc * jax.random.normal(ks[1], (E, H), dtype=jnp.float32), 'gate_bias': sc * jax.random.normal(ks[2], (E,), dtype=jnp.float32), 'Wg': sc * jax.random.normal(ks[3], (E, I, H), dtype=jnp.float32), 'Wu': sc * jax.random.normal(ks[4], (E, I, H), dtype=jnp.float32), 'Wd': sc * jax.random.normal(ks[5], (E, H, I), dtype=jnp.float32), 'Sg': sc * jax.random.normal(ks[6], (S_I, H), dtype=jnp.float32), 'Su': sc * jax.random.normal(ks[7], (S_I, H), dtype=jnp.float32), 'Sd': sc * jax.random.normal(ks[8], (H, S_I), dtype=jnp.float32)}
    _L0_ffn_all = _L0_ffn_setup()
    _L0_ffn_in = {k: v for k, v in _L0_ffn_all.items() if k in ('gate_w', 'gate_bias', 'Wg', 'Wu', 'Wd', 'Sg', 'Su', 'Sd')}
    del _L0_ffn_all

    def _L1_xattn_setup():
        import jax, jax.numpy as jnp
        import numpy as np
        B, TQ, TK, D, H = (2, 1024, 1024, 512, 16)
        HD = D // H
        NUM_PAD = 128
        key = jax.random.key(seed)
        ks = jax.random.split(key, 8)
        s = 0.02
        q = jax.random.normal(ks[0], (B, TQ, D), dtype=jnp.float32)
        kv = jax.random.normal(ks[1], (B, TK, D), dtype=jnp.float32)
        key_padding_mask = jnp.broadcast_to(jnp.arange(TK) >= TK - NUM_PAD, (B, TK))
        Wq = jax.random.normal(ks[2], (D, D), dtype=jnp.float32) * s
        bq = jax.random.normal(ks[3], (D,), dtype=jnp.float32) * s
        Wkv = jax.random.normal(ks[4], (D, 2 * D), dtype=jnp.float32) * s
        bkv = jax.random.normal(ks[5], (2 * D,), dtype=jnp.float32) * s
        Wo = jax.random.normal(ks[6], (D, D), dtype=jnp.float32) * s
        bo = jax.random.normal(ks[7], (D,), dtype=jnp.float32) * s
        return {'q': q, 'kv': kv, 'key_padding_mask': key_padding_mask, 'Wq': Wq, 'bq': bq, 'Wkv': Wkv, 'bkv': bkv, 'Wo': Wo, 'bo': bo}
    _L1_xattn_all = _L1_xattn_setup()
    _L1_xattn_in = {k: v for k, v in _L1_xattn_all.items() if k in ('Wq', 'bq', 'Wkv', 'bkv', 'Wo', 'bo')}
    del _L1_xattn_all

    def _L1_attn_setup():
        import jax, jax.numpy as jnp
        import numpy as np
        DIM = 512
        N_HEADS = 16
        HEAD_DIM = DIM // N_HEADS
        key = jax.random.key(seed)
        ks = jax.random.split(key, 6)
        scale = 1.0 / np.sqrt(DIM)
        inp = jax.random.normal(ks[0], (4, 1024, DIM), dtype=jnp.float32)
        Wq = jax.random.normal(ks[1], (DIM, DIM), dtype=jnp.float32) * scale
        Wk = jax.random.normal(ks[2], (DIM, DIM), dtype=jnp.float32) * scale
        Wv = jax.random.normal(ks[3], (DIM, DIM), dtype=jnp.float32) * scale
        Wo = jax.random.normal(ks[4], (DIM, DIM), dtype=jnp.float32) * scale
        bo = jax.random.normal(ks[5], (DIM,), dtype=jnp.float32) * 0.01
        return {'inp': inp, 'Wq': Wq, 'Wk': Wk, 'Wv': Wv, 'Wo': Wo, 'bo': bo}
    _L1_attn_all = _L1_attn_setup()
    _L1_attn_in = {k: v for k, v in _L1_attn_all.items() if k in ('Wq', 'Wk', 'Wv', 'Wo', 'bo')}
    del _L1_attn_all

    def _L1_ffn_setup():
        import jax, jax.numpy as jnp
        import numpy as np
        INT8_MAX = 127.0

        def _absmax_scale(x, axes):
            amax = jnp.max(jnp.abs(x), axis=axes, keepdims=True)
            return jnp.maximum(amax, 1e-12) / INT8_MAX
        key = jax.random.key(seed)
        k1, k2 = jax.random.split(key)
        lhs = jax.random.normal(k1, (4, 4096, 512), dtype=jnp.float32)
        rhs = jax.random.normal(k2, (512, 512), dtype=jnp.float32)
        return {'lhs': lhs, 'rhs': rhs}
    _L1_ffn_all = _L1_ffn_setup()
    _L1_ffn_in = {k: v for k, v in _L1_ffn_all.items() if k in ('rhs',)}
    del _L1_ffn_all
    return {'x': x, 'ctx_1024': ctx_1024, 'mask_BxS2_bk0': mask_BxS2_bk0, 'L0_xattn_wq': _L0_xattn_in['wq'], 'L0_xattn_bq': _L0_xattn_in['bq'], 'L0_xattn_wk': _L0_xattn_in['wk'], 'L0_xattn_bk': _L0_xattn_in['bk'], 'L0_xattn_wv': _L0_xattn_in['wv'], 'L0_xattn_bv': _L0_xattn_in['bv'], 'L0_xattn_wo': _L0_xattn_in['wo'], 'L0_xattn_bo': _L0_xattn_in['bo'], 'L0_attn_Wq': _L0_attn_in['Wq'], 'L0_attn_Wp': _L0_attn_in['Wp'], 'L0_attn_bp': _L0_attn_in['bp'], 'L0_ffn_gate_w': _L0_ffn_in['gate_w'], 'L0_ffn_gate_bias': _L0_ffn_in['gate_bias'], 'L0_ffn_Wg': _L0_ffn_in['Wg'], 'L0_ffn_Wu': _L0_ffn_in['Wu'], 'L0_ffn_Wd': _L0_ffn_in['Wd'], 'L0_ffn_Sg': _L0_ffn_in['Sg'], 'L0_ffn_Su': _L0_ffn_in['Su'], 'L0_ffn_Sd': _L0_ffn_in['Sd'], 'L1_xattn_Wq': _L1_xattn_in['Wq'], 'L1_xattn_bq': _L1_xattn_in['bq'], 'L1_xattn_Wkv': _L1_xattn_in['Wkv'], 'L1_xattn_bkv': _L1_xattn_in['bkv'], 'L1_xattn_Wo': _L1_xattn_in['Wo'], 'L1_xattn_bo': _L1_xattn_in['bo'], 'L1_attn_Wq': _L1_attn_in['Wq'], 'L1_attn_Wk': _L1_attn_in['Wk'], 'L1_attn_Wv': _L1_attn_in['Wv'], 'L1_attn_Wo': _L1_attn_in['Wo'], 'L1_attn_bo': _L1_attn_in['bo'], 'L1_ffn_rhs': _L1_ffn_in['rhs']}

def reference(x, ctx_1024, mask_BxS2_bk0, L0_xattn_wq, L0_xattn_bq, L0_xattn_wk, L0_xattn_bk, L0_xattn_wv, L0_xattn_bv, L0_xattn_wo, L0_xattn_bo, L0_attn_Wq, L0_attn_Wp, L0_attn_bp, L0_ffn_gate_w, L0_ffn_gate_bias, L0_ffn_Wg, L0_ffn_Wu, L0_ffn_Wd, L0_ffn_Sg, L0_ffn_Su, L0_ffn_Sd, L1_xattn_Wq, L1_xattn_bq, L1_xattn_Wkv, L1_xattn_bkv, L1_xattn_Wo, L1_xattn_bo, L1_attn_Wq, L1_attn_Wk, L1_attn_Wv, L1_attn_Wo, L1_attn_bo, L1_ffn_rhs):
    import jax
    import jax.numpy as jnp

    def _L0_xattn_ref(data, context, wq, bq, wk, bk, wv, bv, wo, bo):
        import jax, jax.numpy as jnp
        import numpy as np
        H = 16
        INPUT_DIM = 512
        FEATURE_DIM = 512
        HEAD_DIM = FEATURE_DIM // H
        B, S1, _ = data.shape
        S2 = context.shape[1]
        q = (data @ wq + bq).reshape(B, S1, H, HEAD_DIM).transpose(0, 2, 1, 3)
        k = (context @ wk + bk).reshape(B, S2, H, HEAD_DIM).transpose(0, 2, 1, 3)
        v = (context @ wv + bv).reshape(B, S2, H, HEAD_DIM).transpose(0, 2, 1, 3)
        scale = 1.0 / np.sqrt(HEAD_DIM).astype(np.float32)
        scores = jnp.einsum('bhqd,bhkd->bhqk', q, k) * scale
        causal = jnp.arange(S1)[:, None] >= jnp.arange(S2)[None, :]
        scores = jnp.where(causal, scores, -jnp.inf)
        probs = jax.nn.softmax(scores, axis=-1)
        z = jnp.einsum('bhqk,bhkd->bhqd', probs, v)
        z = z.transpose(0, 2, 1, 3).reshape(B, S1, FEATURE_DIM)
        return z @ wo + bo

    def _L0_attn_ref(x, Wq, Wp, bp):
        import jax, jax.numpy as jnp
        import numpy as np
        DIM = 512
        NUM_HEADS = 16
        DIM_HEAD = DIM // NUM_HEADS
        NORM = DIM_HEAD ** (-0.5)
        B, N, D = x.shape
        xh = x.reshape(B, N, NUM_HEADS, DIM_HEAD)
        q = jnp.einsum('bnhd,hed->bnhe', xh, Wq)
        scores = jnp.einsum('bnhe,bmhe->bhnm', q, q)
        scores = scores / NORM
        attn = jax.nn.softmax(scores, axis=-1)
        res = jnp.einsum('bhnm,bmhe->bnhe', attn, q)
        y = res.reshape(B, N, D)
        y = y @ Wp.T + bp
        return y

    def _L0_ffn_ref(hidden_states, gate_w, gate_bias, Wg, Wu, Wd, Sg, Su, Sd):
        import jax, jax.numpy as jnp
        import numpy as np
        H = 512
        I = 352
        E = 64
        TOP_K = 8
        NG = 8
        TOPK_GROUP = 4
        N_SHARED = 2
        ROUTED_SCALE = 2.5
        S_I = I * N_SHARED

        def _route(x, gate_w, gate_bias):
            T = x.shape[0]
            logits = x @ gate_w.T
            scores = jax.nn.sigmoid(logits)
            scores_for_choice = scores + gate_bias[None, :]
            grp = scores_for_choice.reshape(T, NG, E // NG)
            group_scores = jnp.sum(jax.lax.top_k(grp, 2)[0], axis=-1)
            _, gidx = jax.lax.top_k(group_scores, TOPK_GROUP)
            gmask = jnp.zeros((T, NG), dtype=scores.dtype).at[jnp.arange(T)[:, None], gidx].set(1.0)
            emask = jnp.repeat(gmask, E // NG, axis=1)
            masked = jnp.where(emask > 0, scores_for_choice, 0.0)
            _, topk_idx = jax.lax.top_k(masked, TOP_K)
            topk_w = jnp.take_along_axis(scores, topk_idx, axis=1)
            topk_w = topk_w / (jnp.sum(topk_w, axis=-1, keepdims=True) + 1e-20)
            topk_w = topk_w * ROUTED_SCALE
            rw = jnp.zeros((T, E), dtype=scores.dtype).at[jnp.arange(T)[:, None], topk_idx].add(topk_w)
            return rw

        def _mlp(x, gw, uw, dw):
            return jax.nn.silu(x @ gw.T) * (x @ uw.T) @ dw.T
        B, S, _ = hidden_states.shape
        x = hidden_states.reshape(B * S, H)
        rw = _route(x, gate_w, gate_bias)
        expert_out = jax.vmap(lambda gw_, uw_, dw_: _mlp(x, gw_, uw_, dw_))(Wg, Wu, Wd)
        routed = jnp.einsum('eth,te->th', expert_out, rw)
        shared = _mlp(x, Sg, Su, Sd)
        out = (routed + shared).reshape(B, S, H)
        return out

    def _L1_xattn_ref(q, kv, key_padding_mask, Wq, bq, Wkv, bkv, Wo, bo):
        import jax, jax.numpy as jnp
        import numpy as np
        B, TQ, TK, D, H = (2, 1024, 1024, 512, 16)
        HD = D // H
        NUM_PAD = 128
        Bc, Tq, Dm = q.shape
        Tk = kv.shape[1]
        scale = HD ** (-0.5)
        Q = (q @ Wq + bq).reshape(Bc, Tq, H, HD).transpose(0, 2, 1, 3)
        KV = (kv @ Wkv + bkv).reshape(Bc, Tk, 2, H, HD).transpose(2, 0, 3, 1, 4)
        K, V = (KV[0], KV[1])
        attn = jnp.einsum('bhqd,bhkd->bhqk', Q, K) * scale
        attn = jnp.where(key_padding_mask[:, None, None, :], -jnp.inf, attn)
        attn = jax.nn.softmax(attn, axis=-1)
        out = jnp.einsum('bhqk,bhkd->bhqd', attn, V)
        out = out.transpose(0, 2, 1, 3).reshape(Bc, Tq, Dm)
        return out @ Wo + bo

    def _L1_attn_ref(inp, Wq, Wk, Wv, Wo, bo):
        import jax, jax.numpy as jnp
        import numpy as np
        DIM = 512
        N_HEADS = 16
        HEAD_DIM = DIM // N_HEADS
        b, s, _ = inp.shape
        q = jnp.einsum('bse,de->bsd', inp, Wq).reshape(b, s, N_HEADS, HEAD_DIM)
        k = jnp.einsum('bse,de->bsd', inp, Wk).reshape(b, s, N_HEADS, HEAD_DIM)
        v = jnp.einsum('bse,de->bsd', inp, Wv).reshape(b, s, N_HEADS, HEAD_DIM)
        scores = jnp.einsum('bqhd,bkhd->bhqk', q, k)
        causal = jnp.triu(jnp.ones((s, s), dtype=bool), k=1)
        scores = jnp.where(causal, -jnp.inf, scores)
        attn = jax.nn.softmax(scores / np.sqrt(HEAD_DIM), axis=-1)
        ctx = jnp.einsum('bhqk,bkhd->bqhd', attn, v).reshape(b, s, DIM)
        return jnp.einsum('bsd,od->bso', ctx, Wo) + bo

    def _L1_ffn_ref(lhs, rhs):
        import jax, jax.numpy as jnp
        import numpy as np
        INT8_MAX = 127.0

        def _absmax_scale(x, axes):
            amax = jnp.max(jnp.abs(x), axis=axes, keepdims=True)
            return jnp.maximum(amax, 1e-12) / INT8_MAX
        lhs_scale = _absmax_scale(lhs, (2,))
        rhs_scale = _absmax_scale(rhs, (0,))
        q_lhs = jnp.clip(jnp.round(lhs / lhs_scale), -INT8_MAX, INT8_MAX).astype(jnp.int8)
        q_rhs = jnp.clip(jnp.round(rhs / rhs_scale), -INT8_MAX, INT8_MAX).astype(jnp.int8)
        acc = jax.lax.dot_general(q_lhs, q_rhs, (((2,), (0,)), ((), ())), preferred_element_type=jnp.int32)
        return acc.astype(jnp.float32) * lhs_scale * rhs_scale
    x = x + _L0_xattn_ref(_layernorm(x, axis=-1), ctx_1024, L0_xattn_wq, L0_xattn_bq, L0_xattn_wk, L0_xattn_bk, L0_xattn_wv, L0_xattn_bv, L0_xattn_wo, L0_xattn_bo)
    x = x + _L0_attn_ref(_layernorm(x, axis=-1), L0_attn_Wq, L0_attn_Wp, L0_attn_bp)
    x = x + _L0_ffn_ref(_layernorm(x, axis=-1), L0_ffn_gate_w, L0_ffn_gate_bias, L0_ffn_Wg, L0_ffn_Wu, L0_ffn_Wd, L0_ffn_Sg, L0_ffn_Su, L0_ffn_Sd)
    x = x + _L1_xattn_ref(_layernorm(x, axis=-1), ctx_1024, mask_BxS2_bk0, L1_xattn_Wq, L1_xattn_bq, L1_xattn_Wkv, L1_xattn_bkv, L1_xattn_Wo, L1_xattn_bo)
    x = x + _L1_attn_ref(_layernorm(x, axis=-1), L1_attn_Wq, L1_attn_Wk, L1_attn_Wv, L1_attn_Wo, L1_attn_bo)
    x = x + _L1_ffn_ref(_layernorm(x, axis=-1), L1_ffn_rhs)
    return x

_drawn_inputs = setup_inputs


def setup_inputs(seed=0):
    import zlib

    import numpy as np

    out = dict(_drawn_inputs(seed))
    spreads = {'L0_xattn_bq': (0.0, 0.1),
     'L0_xattn_bk': (0.0, 2.0),
     'L0_xattn_bv': (0.0, 0.1),
     'L0_xattn_bo': (0.0, 0.1)}
    factors = {'L0_attn_bp': 5.689,
     'L0_ffn_gate_bias': 13.477,
     'L1_xattn_Wq': 6.471,
     'L1_xattn_bq': 173.529,
     'L1_xattn_bkv': 5.879,
     'L1_xattn_bo': 3.743,
     'L1_attn_bo': 6.037,
     'L0_ffn_gate_w': 7.837}
    for name, (base, spread) in spreads.items():
        noise = np.random.default_rng([zlib.crc32(name.encode()), seed]).standard_normal(out[name].shape)
        drawn = base * np.exp(spread * noise) if base else spread * noise
        out[name] = jnp.asarray(drawn.astype(out[name].dtype))
    for name, factor in factors.items():
        out[name] = (out[name] * factor).astype(out[name].dtype)
    return out
```

```python
from contextlib import ExitStack

import numpy as np
import concourse.bass as bass
from concourse import mybir

F32 = mybir.dt.float32
BF16 = mybir.dt.bfloat16
I32 = mybir.dt.int32
U32 = mybir.dt.uint32
U8 = mybir.dt.uint8
ALU = mybir.AluOpType
ACT = mybir.ActivationFunctionType
AX = mybir.AxisListType
RMAX = bass.bass_isa.ReduceOp.max

P = 128
B, S1, D, S2 = 8, 64, 512, 1601
T = B * S1
NT = T // P
NC = D // P
H, HD = 16, 32
NP = H // 2
E, I, TOPK, NG, TG = 64, 352, 8, 8, 4
NE = E + 2
MAXT = (T * TOPK + E * (P - 1)) // P
NCOL = MAXT + 1
IJ = [(0, 128), (128, 128), (256, 96)]
KC = [(0, 512), (512, 512), (1024, 512), (1536, 65)]
KT_N = 13
EPS = 1e-5
NEG = -1e30
ROUND = 12582912.0
SC = float(HD) ** -0.5
ROUTED_SCALE = 2.5


def perceiver(nc, a, out):
    acc = nc.dram_tensor("moe_acc", (T + P, D), F32, kind="Internal").ap()
    xrow = nc.dram_tensor("moe_rows", (T + P, D), F32, kind="Internal").ap()

    with ExitStack() as ctx:
        def sb(name, shape, dt=F32):
            return ctx.enter_context(nc.sbuf_tensor(name, shape, dt))

        def sem(name):
            return ctx.enter_context(nc.semaphore(name))

        x = sb("x", [P, NT, D])
        xn = sb("xn", [P, NT, D])
        xnT = sb("xnT", [P, NC, T])
        zT = xnT[:, :, :].rearrange("p (jj h) t -> p jj h t", jj=2)
        slot = [sb(f"wslot{i}", [P, NC, D]) for i in range(4)]
        qbd = sb("qbd", [P, NC, B, P])
        z = sb("z", [P, 2, NP, HD])
        ident = sb("ident", [P, P])
        causal = sb("causal", [P, S1])
        halfmask = sb("halfmask", [P, 2])
        bias_c = sb("bias_c", [P, 4, NC])
        bias_r = sb("bias_r", [P, D])
        vbias = sb("vbias", [P, D])
        gbias = sb("gbias", [P, E])
        wbd = sb("wbd", [P, NC, P])
        wsmall = sb("wsmall", [P, NC, HD])
        gatew = sb("gatew", [P, NC, E])
        st = sb("st", [P, NT, 6])
        mv = sb("mv", [P, NT, 2])
        rstd = sb("rstd", [P, NT])
        neg_half = sb("neg_half", [P, NT])
        smx = sb("smx", [P, 2, 16])
        ssum = sb("ssum", [P, 16])
        rinv = sb("rinv", [P, 16])
        mask8 = sb("mask8", [P, S2], U8)
        maskadd = sb("maskadd", [P, S2], BF16)
        R0 = sb("R0", [P, 13400])
        R1 = sb("R1", [P, 14200])
        PS = ctx.enter_context(nc.psum_tensor("PS", [P, 8, 512], F32))

        class Arena:

            def __init__(self, region, at=0):
                self.region, self.at = region, at

            def view(self, *dims):
                n = int(np.prod(dims))
                v = self.region[:, self.at:self.at + n]
                self.at += n
                if len(dims) == 1:
                    return v
                names = "abcd"[:len(dims)]
                return v.rearrange(f"p ({' '.join(names)}) -> p {' '.join(names)}",
                                   **{k: d for k, d in zip(names, dims)})

        m = Arena(R1)
        kT = m.view(NC, T)
        v64 = m.view(NT, D)
        s64 = [m.view(NP, 2, S1) for _ in range(2)]
        pT64 = m.view(NP, P)
        ctx0 = m.view(NC, T)
        m = Arena(R0)
        wgu = [m.view(NC, 2, I) for _ in range(2)]
        wdn = [m.view(3, D) for _ in range(2)]
        xg = [m.view(D) for _ in range(2)]
        xgT = [m.view(NC, P) for _ in range(2)]
        act_g = m.view(I)
        hid = m.view(I)
        hT = m.view(3, P)
        yrow = [m.view(D) for _ in range(2)]
        assert m.at <= 13400, m.at
        sgate = [xg[k][:, 0:I] for k in range(2)]
        shid = [yrow[k][:, 0:I] for k in range(2)]
        shT = hT
        m = Arena(R1)
        iota128 = m.view(P)
        upper = m.view(P)
        ones = m.view(P)
        zero512 = m.view(D)
        scores = m.view(NT, E)
        choice = m.view(NT, E)
        tmp64 = m.view(NT, E)
        srt = m.view(NT, NG, 8)
        gsum = m.view(NT, NG)
        gtop = m.view(NT, 8)
        gidx = m.view(NT, 8).bitcast(U32)
        gidxf = m.view(NT, 8)
        eqg = m.view(NT, NG, TG)
        gmask = m.view(NT * NG)
        top8 = m.view(NT, 8)
        idx8 = m.view(NT, 8).bitcast(U32)
        idx8f = m.view(NT * 8)
        eq = m.view(NT, 8, E)
        eqt = m.view(NT, 8, E)
        sel = m.view(NT, E)
        slotm = m.view(NT, E)
        wsum = m.view(NT)
        wnorm = m.view(NT)
        wk = m.view(NT * 8)
        slk = m.view(NT * 8)
        sdiv = m.view(NT * 8)
        smod = m.view(NT * 8)
        tokv = m.view(NT * 8)
        cnt = m.view(E)
        ntile = m.view(E)
        cum = m.view(E)
        base = m.view(E)
        cmp64 = m.view(E)
        oneA = [m.view(8, P) for _ in range(2)]
        eqB = m.view(8, NCOL)
        twoB = [m.view(8, 2, NCOL) for _ in range(2)]
        assert m.at <= 14200, m.at
        iotap = sb("iotap", [P, 1])
        pad_row = sb("pad_row", [P, 1])
        tok_id = sb("tok_id", [P, NT])
        idx_tab = sb("idx_tab", [P, NCOL], I32)
        w_tab = sb("w_tab", [P, NCOL])
        gcol = sb("gcol", [P, 1], I32)
        scol = sb("scol", [P, 1], I32)
        eot = sb("eot", [P, 2])
        eot_row = sb("eot_row", [1, P], I32)
        n_iter = sb("n_iter", [1, 1], I32)
        m = Arena(R0)
        kTx = [m.view(2, S2) for _ in range(2)]
        vx = [m.view(KT_N, D // 2) for _ in range(2)]
        assert m.at <= 13400, m.at
        m = Arena(R1)
        ctxT = m.view(NC, S2)
        wkv = m.view(NC, 2 * D)
        sx = [m.view(S2) for _ in range(2)]
        assert m.at <= 14200, m.at
        pTx = [sb(f"pTx{i}", [P, 4, P]) for i in range(2)]
        qbh = [sb(f"qbh{i}", [P, 2, P]) for i in range(2)]
        mx4 = sb("mx4", [P, 4])
        nmx = sb("nmx", [P, 2])
        rsx = sb("rsx", [P, 2])
        rix = sb("rix", [P, 2])
        m = Arena(R0)
        rhs = m.view(NC, D)
        rabs = m.view(D)
        rscale = m.view(D)
        lscale = m.view(NT)
        linv = m.view(NT)
        rtmp = m.view(NC, D)
        rq = m.view(NC, D // 2).bitcast(BF16)
        lq = m.view(NC, T // 2).bitcast(BF16)

        ld_x = sem("ld_x"); ld_l0kv = sem("ld_l0kv"); ld_l0q = sem("ld_l0q"); ld_l0o = sem("ld_l0o")
        ld_bias = sem("ld_bias"); ld_small = sem("ld_small"); ld_p = sem("ld_p"); ld_boa = sem("ld_boa")
        ld_gate = sem("ld_gate"); ld_sh = sem("ld_sh"); ld_l1q = sem("ld_l1q"); ld_l1o = sem("ld_l1o")
        ld_l1a = sem("ld_l1a"); ld_l1ao = sem("ld_l1ao"); ld_bo1 = sem("ld_bo1"); ld_boa1 = sem("ld_boa1")
        ld_rhs = sem("ld_rhs"); ld_wkv = sem("ld_wkv"); ld_vb1 = sem("ld_vb1")
        consts = sem("consts"); pool_seq = sem("pool_seq"); dve_seq = sem("dve_seq"); act_seq = sem("act_seq")
        mv_ready = sem("mv_ready"); rstd_ready = sem("rstd_ready"); xn_ready = sem("xn_ready"); xt_made = sem("xt_made"); xT_ready = sem("xT_ready")
        xb_ready = sem("xb_ready"); q_made = sem("q_made"); q_ready = sem("q_ready")
        k_made = sem("k_made"); k_ready = sem("k_ready"); v_made = sem("v_made"); v_ready = sem("v_ready")
        sc_made = sem("sc_made"); sm_ready = sem("sm_ready"); p_ready = sem("p_ready")
        pt_made = sem("pt_made"); pt_act = sem("pt_act"); pt_dve = sem("pt_dve"); pv_made = sem("pv_made")
        z_ready = sem("z_ready"); zt_made = sem("zt_made"); zt_ready = sem("zt_ready")
        pj_made = sem("pj_made"); x_ready = sem("x_ready")
        wbd_ready = sem("wbd_ready"); zpad_set = sem("zpad_set"); rix_ready = sem("rix_ready"); dve_x = sem("dve_x")
        dve_seq3 = sem("dve_seq3"); dve_seq4 = sem("dve_seq4"); pool_seq4 = sem("pool_seq4")
        ff_x = sem("ff_x"); ff_y = sem("ff_y")
        lg_made = sem("lg_made"); lg_exp = sem("lg_exp"); sel_ready = sem("sel_ready"); rank_made = sem("rank_made")
        ab_ready = sem("ab_ready"); tab_made = sem("tab_made"); eot_ready = sem("eot_ready")
        eot_made = sem("eot_made"); tables = sem("tables"); rows_out = sem("rows_out"); acc_out = sem("acc_out")
        sh_g = sem("sh_g"); sh_u = sem("sh_u"); sh_silu = sem("sh_silu"); sh_h = sem("sh_h")
        sh_t = sem("sh_t"); sh_ht = sem("sh_ht"); sh_d = sem("sh_d"); sh_y = sem("sh_y")
        w_gu = [sem(f"w_gu{k}") for k in range(2)]; w_dn = [sem(f"w_dn{k}") for k in range(2)]; g_made = sem("g_made"); u_made = sem("u_made")
        silu_ready = sem("silu_ready"); h_ready = sem("h_ready"); ht_made = sem("ht_made")
        ht_ready = sem("ht_ready"); xg_loaded = [sem(f"xg_loaded{k}") for k in range(2)]; xg_made = sem("xg_made")
        xg_ready = sem("xg_ready"); y_made = sem("y_made"); y_ready = sem("y_ready"); y_added = sem("y_added")
        gcol_set = sem("gcol_set"); scol_set = sem("scol_set"); acc_in = sem("acc_in")
        ctx_ld = [sem(f"ctx_ld{c}") for c in range(4)]
        ctx_free = sem("ctx_free"); mask_ld = sem("mask_ld"); mask_set = sem("mask_set")
        kx_made = sem("kx_made"); kx_ready = sem("kx_ready"); vx_made = sem("vx_made"); vx_ready = sem("vx_ready")
        qh_ready = sem("qh_ready"); sx_made = sem("sx_made"); sx_read = sem("sx_read"); sx_max = sem("sx_max")
        px_ready = sem("px_ready"); ptx_made = sem("ptx_made"); ptx_act = sem("ptx_act"); ptx_dve = sem("ptx_dve")
        pvx_part = sem("pvx_part"); pvx_made = sem("pvx_made"); zx_ready = sem("zx_ready")
        ztx_made = sem("ztx_made"); ztx_ready = sem("ztx_ready"); px_l1 = sem("px_l1"); xx_ready = sem("xx_ready")
        rq_ready = sem("rq_ready"); lq_made = sem("lq_made"); lq_ready = sem("lq_ready")
        ff_made = sem("ff_made"); rabs_ready = sem("rabs_ready"); rmax_ready = sem("rmax_ready"); out_done = sem("out_done")
        pj1_made = sem("pj1_made")

        class Chain:

            def __init__(self, eng, s):
                self.eng, self.s, self.n = eng, s, 0

            def __call__(self, ins):
                ins.then_inc(self.s, 1)
                self.n += 1
                self.eng.wait_ge(self.s, self.n)

        def count(eng, value):
            return value if isinstance(value, int) else eng.snap(eng.to_reg(value))


        def ln_dve(dve, link, n):
            for t in range(NT):
                last = nc.vector.bn_stats(st[:, t, :], x[:, t, :])
            link(last)
            for t in range(NT):
                last = nc.vector.bn_aggr(mv[:, t, :], st[:, t, :])
            link(last)
            nc.vector.tensor_scalar(rstd[:, :], mv[:, :, 1], EPS, None, ALU.add).then_inc(mv_ready, 1)
            dve.wait_ge(rstd_ready, n + 1)
            for t in range(NT):
                nc.vector.tensor_scalar(xn[:, t, :], x[:, t, :], mv[:, t, 0:1], rstd[:, t:t + 1],
                                        ALU.subtract, ALU.mult).then_inc(xn_ready, 1)

        def ln_pool(pool, n):
            pool.wait_ge(mv_ready, n + 1)
            nc.gpsimd.tensor_tensor(rstd[:, :], rstd[:, :], neg_half[:, :], ALU.pow).then_inc(rstd_ready, 1)

        def xt_pe(pe, n):
            for t in range(NT):
                pe.wait_ge(xn_ready, NT * n + t + 1)
                for c in range(NC):
                    last = nc.tensor.transpose(PS[:, t, c * P:(c + 1) * P], xn[:, t, c * P:(c + 1) * P], ident[:, :])
                last.then_inc(xt_made, 1)

        def xt_copy(eng, copy, n, tiles):
            for t in tiles:
                eng.wait_ge(xt_made, NT * n + t + 1)
                copy(xnT[:, :, t * P:(t + 1) * P],
                     PS[:, t, :].rearrange("p (c k) -> p c k", c=NC)).then_inc(xT_ready, 1)

        def q_pe(pe, w, n, L):
            pe.wait_ge(xT_ready, NT * (n + 1))
            for dc in range(NC):
                for c in range(NC):
                    last = nc.tensor.matmul(PS[:, 4 + dc, :], w[:, c, dc * P:(dc + 1) * P], xnT[:, c, :],
                                            start=(c == 0), stop=(c == NC - 1))
                last.then_inc(q_made, 1)

        def q_dve(dve, L, bias):
            for dc in range(NC):
                dve.wait_ge(q_made, NC * L + dc + 1)
                src = PS[:, 4 + dc, :].rearrange("p (b q) -> p b q", b=B)
                for h in range(2):
                    dst = qbd[:, dc, :, h * S1:(h + 1) * S1]
                    if bias is None:
                        last = nc.vector.tensor_scalar(dst, src, halfmask[:, h:h + 1], None, ALU.mult)
                    else:
                        last = nc.vector.tensor_scalar(dst, src, bias_c[:, bias, dc:dc + 1], halfmask[:, h:h + 1],
                                                       ALU.add, ALU.mult)
                last.then_inc(q_ready, 1)

        def att_pe(pe, L, wo):
            def sc(t):
                b0 = 2 * (t % 2)
                if t >= 2:
                    pe.wait_ge(sm_ready, L * NT + t - 1)
                for par in range(2):
                    b = 2 * t + par
                    for m in range(NP):
                        r, dc = 64 * (m // 4), m % 4
                        c0 = (2 * dc + par) * S1
                        last = nc.tensor.matmul(PS[:, b0 + m // 4, c0:c0 + S1],
                                                qbd[r:r + 64, dc, b, :], kT[r:r + 64, dc, b * S1:(b + 1) * S1],
                                                start=True, stop=True)
                last.then_inc(sc_made, 1)

            sc(0)
            sc(1)
            for t in range(NT):
                k = L * NT + t + 1
                pe.wait_ge(p_ready, k)
                for pr in range(NP):
                    last = nc.tensor.transpose(PS[:, 4 + pr // 4, (pr % 4) * P:(pr % 4 + 1) * P],
                                               s64[t % 2][:, pr, :, :].rearrange("p a b -> p (a b)"), ident[:, :])
                    if pr % 4 == 3:
                        last.then_inc(pt_made, 1)
                pe.wait_ge(pt_act, k)
                pe.wait_ge(pt_dve, k)
                for par in range(2):
                    for m in range(NP):
                        v0 = (2 * (m % 4) + m // 4) * 64
                        last = nc.tensor.matmul(PS[:, 6 + par, m * 64:(m + 1) * 64],
                                                pT64[64 * par:64 * par + 64, m, :],
                                                v64[64 * par:64 * par + 64, t, v0:v0 + 64],
                                                start=True, stop=True)
                last.then_inc(pv_made, 1)
                if t + 2 < NT:
                    sc(t + 2)
                pe.wait_ge(z_ready, k)
                for par in range(2):
                    for jj in range(2):
                        last = nc.tensor.transpose(PS[:, 4, (2 * par + jj) * P:(2 * par + jj + 1) * P],
                                                   z[:, par, 4 * jj:4 * jj + 4, :].rearrange("p a b -> p (a b)"),
                                                   ident[:, :])
                last.then_inc(zt_made, 1)
                pe.wait_ge(zt_ready, k)
                for jh in range(4):
                    last = nc.tensor.matmul(PS[:, 5, :], zT[:, jh // 2, jh % 2, t * P:(t + 1) * P], wo[:, jh, :],
                                            start=(jh == 0), stop=(jh == 3))
                last.then_inc(pj_made, 1)
                if t + 1 < NT:
                    pe.wait_ge(x_ready, k)

        def att_act(act, L, scale):
            def ex(t):
                act.wait_ge(sm_ready, L * NT + t + 1)
                sv = s64[t % 2].rearrange("p a b c -> p (a b c)")
                nc.scalar.activation(sv, sv, ACT.Exp, scale=scale).then_inc(p_ready, 1)

            ex(0)
            ex(1)
            for t in range(NT):
                k = L * NT + t + 1
                act.wait_ge(pt_made, 2 * (k - 1) + 1)
                nc.scalar.copy(pT64[:, 0:4, :].rearrange("p a b -> p (a b)"), PS[:, 4, :]).then_inc(pt_act, 1)
                act.wait_ge(zt_made, k)
                for par in range(2):
                    b = 2 * t + par
                    last = nc.scalar.copy(
                        zT[:, :, :, b * S1:(b + 1) * S1],
                        PS[:, 4, par * 256:(par + 1) * 256].rearrange("p (j h q) -> p j h q", j=2, h=2))
                last.then_inc(zt_ready, 1)
                if t + 2 < NT:
                    ex(t + 2)

        def att_dve(dve, link, L, masked):
            def pre(t):
                dve.wait_ge(sc_made, L * NT + t + 1)
                src = PS[:, 2 * (t % 2):2 * (t % 2) + 2, :].rearrange("p a (r b k) -> p (a r) b k", b=2, k=S1)
                s, mx = s64[t % 2], smx[:, t % 2, :].rearrange("p (a b) -> p a b", a=NP)
                if masked:
                    link(nc.vector.tensor_tensor(s, src, causal[:, :].unsqueeze(1).unsqueeze(1)
                                                 .to_broadcast([P, NP, 2, S1]), ALU.add))
                    src = s
                link(nc.vector.tensor_reduce(mx, src, AX.X, ALU.max))
                nc.vector.tensor_tensor(s, src, mx.unsqueeze(3).to_broadcast([P, NP, 2, S1]),
                                        ALU.subtract).then_inc(sm_ready, 1)

            pre(0)
            pre(1)
            for t in range(NT):
                k = L * NT + t + 1
                dve.wait_ge(p_ready, k)
                link(nc.vector.tensor_reduce(ssum[:, :].rearrange("p (a b) -> p a b", a=NP), s64[t % 2],
                                             AX.X, ALU.add))
                link(nc.vector.reciprocal(rinv[:, :], ssum[:, :]))
                dve.wait_ge(pt_made, 2 * k)
                nc.vector.tensor_copy(pT64[:, 4:8, :].rearrange("p a b -> p (a b)"), PS[:, 5, :]).then_inc(pt_dve, 1)
                dve.wait_ge(pv_made, k)
                for h in range(2):
                    r = slice(64 * h, 64 * h + 64)
                    last = nc.vector.tensor_tensor(
                        z[r, :, :, :],
                        PS[r, 6:8, :].rearrange("p a (r h d) -> p a r h d", h=2, d=HD)[:, :, :, h, :],
                        rinv[r, :].rearrange("p (r a) -> p a r", a=2).unsqueeze(3).to_broadcast([64, 2, NP, HD]),
                        ALU.mult)
                last.then_inc(z_ready, 1)
                if t + 2 < NT:
                    pre(t + 2)
                dve.wait_ge(pj_made, k)
                dve.wait_ge(xb_ready, XB[L])
                nc.vector.tensor_tensor(x[:, t, :], x[:, t, :], PS[:, 5, :], ALU.add).then_inc(x_ready, 1)
            dve.wait_ge(x_ready, (L + 1) * NT)

        XB = [1, 2, 4]

        def add_out_bias(pool, n, after):
            pool.wait_ge(xn_ready, NT * after)
            nc.gpsimd.tensor_tensor(x[:, :, :], x[:, :, :],
                                    bias_r[:, :].unsqueeze(1).to_broadcast([P, NT, D]), ALU.add).then_inc(xb_ready, 1)

        with nc.Block() as block:
            @block.sync
            def _(sp):
                sp.dma_start(ctx0, a["ctx0"]).then_inc(ld_l0kv, 16)
                sp.dma_start(slot[1][:, :, :], a["l0_wk"]).then_inc(ld_l0kv, 16)
                sp.dma_start(bias_c[:, :, :], a["bias_c"]).then_inc(ld_bias, 16)
                sp.dma_start(x[:, :, :], a["x"]).then_inc(ld_x, 16)
                sp.dma_start(slot[2][:, :, :], a["l0_wv"]).then_inc(ld_l0kv, 16)
                sp.dma_start(vbias[:, :], a["l0_bv"].to_broadcast([P, D])).then_inc(ld_bias, 16)
                sp.dma_start(slot[0][:, :, :], a["l0_wq"]).then_inc(ld_l0q, 16)
                sp.dma_start(bias_r[:, :], a["l0_bo"].to_broadcast([P, D])).then_inc(ld_bias, 16)
                sp.dma_start(slot[3][:, :, :], a["l0_wo"]).then_inc(ld_l0o, 16)
                sp.dma_start(wsmall[:, :, :], a["l0a_wq"]).then_inc(ld_small, 16)
                sp.dma_start(gatew[:, :, :], a["gate_w"]).then_inc(ld_gate, 16)
                sp.dma_start(gbias[:, :], a["gate_b"].to_broadcast([P, E])).then_inc(ld_gate, 16)
                for k in range(2):
                    sp.dma_start(wgu[k], a["w_gu"][E + k]).then_inc(ld_sh, 16)
                    sp.dma_start(wdn[k][:, 0:2, :], a["w_dna"][E + k]).then_inc(ld_sh, 16)
                    sp.dma_start(wdn[k][0:96, 2, :], a["w_dnb"][E + k]).then_inc(ld_sh, 16)
                sp.wait_ge(k_made, NC)
                sp.dma_start(slot[1][:, :, :], a["l0a_wp"]).then_inc(ld_p, 16)
                sp.wait_ge(q_made, NC)
                sp.dma_start(slot[0][:, :, :], a["l1_wq"]).then_inc(ld_l1q, 16)
                sp.wait_ge(v_made, NT)
                sp.dma_start(slot[2][:, :, :], a["l1_wo"]).then_inc(ld_l1o, 16)
                sp.wait_ge(xb_ready, 1)
                sp.dma_start(bias_r[:, :], a["l0a_bp"].to_broadcast([P, D])).then_inc(ld_boa, 16)
                sp.wait_ge(pj_made, NT)
                sp.dma_start(slot[3][:, :, :], a["l1a_wq"]).then_inc(ld_l1a, 16)
                sp.wait_ge(pj_made, 2 * NT)
                sp.dma_start(slot[1][:, :, :], a["l1a_wv"]).then_inc(ld_l1a, 16)
                sp.wait_ge(consts, 1)
                sp.wait_ge(xn_ready, 3 * NT)
                sp.wait_ge(zpad_set, 1)
                sp.dma_start(xrow[0:T, :].rearrange("(t p) d -> p t d", p=P), xn[:, :, :]).then_inc(rows_out, 16)
                sp.dma_start(xrow[T:T + P, :], zero512).then_inc(rows_out, 16)
                sp.dma_start(acc[T:T + P, :], zero512).then_inc(acc_out, 16)
                sp.wait_ge(sh_y, NT)
                sp.dma_start(acc[0:T, :].rearrange("(t p) d -> p t d", p=P), x[:, :, :]).then_inc(acc_out, 16)
                sp.wait_ge(rows_out, 32)
                sp.wait_ge(acc_out, 32)

            @block.gpsimd
            def _(pool):
                link = Chain(pool, pool_seq)
                link(nc.gpsimd.memset(neg_half[:, :], -0.5))
                link(nc.gpsimd.memset(ident[:, :], 0.0))
                link(nc.gpsimd.affine_select(out=ident[:, :], in_=ident[:, :], compare_op=ALU.not_equal, fill=1.0,
                                             base=0, pattern=[[-1, P]], channel_multiplier=1))
                link(nc.gpsimd.memset(causal[:, :], 0.0))
                for h in range(2):
                    r = slice(64 * h, 64 * h + 64)
                    link(nc.gpsimd.affine_select(out=causal[r, :], in_=causal[r, :], compare_op=ALU.is_ge, fill=NEG,
                                                 base=0, pattern=[[-1, S1]], channel_multiplier=1))
                for g in range(4):
                    r = slice(32 * g, 32 * g + 32)
                    link(nc.gpsimd.memset(halfmask[r, 0:1], 1.0 - g % 2))
                    link(nc.gpsimd.memset(halfmask[r, 1:2], float(g % 2)))
                link(nc.gpsimd.memset(wbd[:, :, :], 0.0))
                link(nc.gpsimd.iota(iotap[:, :], [[0, 1]], base=0, channel_multiplier=1,
                                    allow_small_or_imprecise_dtypes=True))
                link(nc.gpsimd.iota(pad_row[:, :], [[0, 1]], base=T, channel_multiplier=1,
                                    allow_small_or_imprecise_dtypes=True))
                link(nc.gpsimd.iota(tok_id[:, :], [[P, NT]], base=-T, channel_multiplier=1,
                                    allow_small_or_imprecise_dtypes=True))
                nc.gpsimd.memset(eot[:, :], 0.0).then_inc(consts, 1)
                ln_pool(pool, 0)
                pool.wait_ge(ld_small, 16)
                for g in range(4):
                    r = slice(32 * g, 32 * g + 32)
                    nc.gpsimd.tensor_copy(wbd[r, :, 32 * g:32 * g + 32], wsmall[r, :, :]).then_inc(wbd_ready, 1)
                    pool.wait_ge(wbd_ready, g + 1)
                pool.wait_ge(ld_bias, 48)
                add_out_bias(pool, 0, 1)
                ln_pool(pool, 1)
                pool.wait_ge(ld_boa, 16)
                add_out_bias(pool, 1, 2)
                ln_pool(pool, 2)
                pool.wait_ge(pj_made, 2 * NT)
                link(nc.gpsimd.iota(iota128, [[1, P]], base=0, channel_multiplier=0,
                                    allow_small_or_imprecise_dtypes=True))
                link(nc.gpsimd.memset(ones, 1.0))
                link(nc.gpsimd.memset(upper, 1.0))
                link(nc.gpsimd.affine_select(out=upper, in_=upper, compare_op=ALU.is_gt, fill=0.0,
                                             base=0, pattern=[[1, P]], channel_multiplier=-1))
                nc.gpsimd.memset(zero512, 0.0).then_inc(zpad_set, 1)

            @block.tensor
            def _(pe):
                pe.wait_ge(ld_l0kv, 48)
                for dc in range(NC):
                    for c in range(NC):
                        last = nc.tensor.matmul(PS[:, dc, :], slot[1][:, c, dc * P:(dc + 1) * P], ctx0[:, c, :],
                                                start=(c == 0), stop=(c == NC - 1))
                    last.then_inc(k_made, 1)
                for t in range(NT):
                    for c in range(NC):
                        last = nc.tensor.matmul(PS[:, 4 + t, :], ctx0[:, c, t * P:(t + 1) * P], slot[2][:, c, :],
                                                start=(c == 0), stop=(c == NC - 1))
                    last.then_inc(v_made, 1)
                pe.wait_ge(consts, 1)
                pe.wait_ge(k_ready, NC)
                xt_pe(pe, 0)
                pe.wait_ge(v_ready, NT)
                pe.wait_ge(ld_l0q, 16)
                q_pe(pe, slot[0], 0, 0)
                pe.wait_ge(q_ready, NC)
                pe.wait_ge(ld_l0o, 16)
                att_pe(pe, 0, slot[3])

                xt_pe(pe, 1)
                pe.wait_ge(xT_ready, 2 * NT)
                pe.wait_ge(wbd_ready, 4)
                for dc in range(NC):
                    nc.tensor.matmul(PS[:, 4 + dc, :], wbd[:, dc, :], xnT[:, dc, :],
                                     start=True, stop=True).then_inc(q_made, 1)
                for t in range(NT):
                    for dc in range(NC):
                        last = nc.tensor.matmul(PS[:, t, dc * P:(dc + 1) * P], xnT[:, dc, t * P:(t + 1) * P],
                                                wbd[:, dc, :], start=True, stop=True)
                    last.then_inc(v_made, 1)
                pe.wait_ge(q_ready, 2 * NC)
                pe.wait_ge(v_ready, 2 * NT)
                pe.wait_ge(ld_p, 16)
                att_pe(pe, 1, slot[1])

                xt_pe(pe, 2)
                pe.wait_ge(xT_ready, 3 * NT)
                pe.wait_ge(ld_gate, 32)
                for t in range(NT):
                    for c in range(NC):
                        last = nc.tensor.matmul(PS[:, 0, t * E:(t + 1) * E], xnT[:, c, t * P:(t + 1) * P],
                                                gatew[:, c, :], start=(c == 0), stop=(c == NC - 1))
                last.then_inc(lg_made, 1)

                def shared_in(k):
                    t, hf = k // 2, k % 2
                    if k >= 2:
                        pe.wait_ge(sh_silu, k - 1)
                        pe.wait_ge(sh_h, k - 1)
                    for gu in range(2):
                        for c in range(NC):
                            last = nc.tensor.matmul(PS[:, 2 + 2 * hf + gu, 0:I], xnT[:, c, t * P:(t + 1) * P],
                                                    wgu[hf][:, c, gu, :], start=(c == 0), stop=(c == NC - 1))
                        last.then_inc(sh_u if gu else sh_g, 1)

                def shared_out(k):
                    t, hf = k // 2, k % 2
                    pe.wait_ge(sh_h, k + 1)
                    if k >= 1:
                        pe.wait_ge(sh_ht, k)
                    for j, (i0, n) in enumerate(IJ):
                        last = nc.tensor.transpose(PS[0:n, 6, j * P:(j + 1) * P], shid[hf][:, i0:i0 + n], ident[:, :])
                    last.then_inc(sh_t, 1)
                    pe.wait_ge(sh_ht, k + 1)
                    if hf == 0 and t >= 1:
                        pe.wait_ge(sh_y, t)
                    for j, (i0, n) in enumerate(IJ):
                        last = nc.tensor.matmul(PS[:, 7, :], shT[0:n, j, :], wdn[hf][0:n, j, :],
                                                start=(hf == 0 and j == 0), stop=(hf == 1 and j == 2))
                    last.then_inc(sh_d, 1)

                pe.wait_ge(ld_sh, 96)
                shared_in(0)
                shared_in(1)
                shared_out(0)
                shared_in(2)
                shared_out(1)
                shared_in(3)
                shared_out(2)
                pe.wait_ge(sel_ready, 1)
                for t in range(NT):
                    for u in range(t + 1):
                        nc.tensor.matmul(PS[:, 0, t * E:(t + 1) * E], ones if u < t else upper, sel[:, u, :],
                                         start=(u == 0), stop=(u == t))
                for u in range(NT):
                    last = nc.tensor.matmul(PS[:, 0, NT * E:(NT + 1) * E], ones, sel[:, u, :],
                                            start=(u == 0), stop=(u == NT - 1))
                last.then_inc(rank_made, 1)
                shared_in(4)
                shared_out(3)
                shared_in(5)
                shared_out(4)
                pe.wait_ge(eot_ready, 1)
                nc.tensor.transpose(PS[0:2, 0, 0:P], eot[:, :], ident[:, :]).then_inc(eot_made, 1)
                shared_in(6)
                shared_out(5)
                shared_in(7)
                shared_out(6)
                for t in range(NT):
                    pe.wait_ge(ab_ready, t + 1)
                    for k in range(8):
                        last = nc.tensor.matmul(PS[:, 1, 0:2 * NCOL], oneA[t % 2][:, k, :],
                                                twoB[t % 2][:, k, :, :].rearrange("p a b -> p (a b)"),
                                                start=(t == 0 and k == 0), stop=(t == NT - 1 and k == 7))
                    last.then_inc(tab_made, 1)
                shared_out(7)

            def shared_ht(act, k):
                act.wait_ge(sh_t, k + 1)
                if k >= 1:
                    act.wait_ge(sh_d, k)
                nc.scalar.copy(shT[:, 0:2, :], PS[:, 6, 0:2 * P].rearrange("p (a b) -> p a b", a=2))
                nc.scalar.copy(shT[0:96, 2, :], PS[0:96, 6, 2 * P:3 * P]).then_inc(sh_ht, 1)

            @block.scalar
            def _(act):
                act.wait_ge(ld_bias, 48)
                for dc in range(NC):
                    act.wait_ge(k_made, dc + 1)
                    nc.scalar.activation(kT[:, dc, :], PS[:, dc, :], ACT.Identity,
                                         bias=bias_c[:, 1, dc:dc + 1]).then_inc(k_ready, 1)
                xt_copy(act, nc.scalar.copy, 0, (0, 2))
                att_act(act, 0, SC)
                xt_copy(act, nc.scalar.copy, 1, (0, 2))
                for dc in range(NC):
                    act.wait_ge(q_made, NC + dc + 1)
                    nc.scalar.copy(kT[:, dc, :], PS[:, 4 + dc, :]).then_inc(k_ready, 1)
                for t in range(NT):
                    act.wait_ge(v_made, NT + t + 1)
                    nc.scalar.copy(v64[:, t, :], PS[:, t, :]).then_inc(v_ready, 1)
                att_act(act, 1, 1.0 / SC)
                xt_copy(act, nc.scalar.copy, 2, (0, 2))
                act.wait_ge(lg_made, 1)
                nc.scalar.activation(scores.rearrange("p a b -> p (a b)"), PS[:, 0, 0:NT * E], ACT.Exp,
                                     scale=-1.0).then_inc(lg_exp, 1)
                for k in range(2 * NT):
                    hf = k % 2
                    act.wait_ge(sh_g, k + 1)
                    if k >= 2:
                        act.wait_ge(sh_h, k - 1)
                    nc.scalar.activation(sgate[hf], PS[:, 2 + 2 * hf, 0:I], ACT.Silu).then_inc(sh_silu, 1)
                    if k >= 1:
                        shared_ht(act, k - 1)
                shared_ht(act, 2 * NT - 1)

            @block.vector
            def _(dve):
                link = Chain(dve, dve_seq)
                dve.wait_ge(ld_x, 16)
                ln_dve(dve, link, 0)
                dve.wait_ge(ld_bias, 48)
                for t in range(NT):
                    dve.wait_ge(v_made, t + 1)
                    nc.vector.tensor_tensor(v64[:, t, :], PS[:, 4 + t, :], vbias[:, :], ALU.add).then_inc(v_ready, 1)
                xt_copy(dve, nc.vector.tensor_copy, 0, (1, 3))
                dve.wait_ge(consts, 1)
                q_dve(dve, 0, 0)
                att_dve(dve, link, 0, True)

                ln_dve(dve, link, 1)
                xt_copy(dve, nc.vector.tensor_copy, 1, (1, 3))
                for dc in range(NC):
                    dve.wait_ge(k_ready, NC + dc + 1)
                    for h in range(2):
                        last = nc.vector.tensor_scalar(qbd[:, dc, :, h * S1:(h + 1) * S1],
                                                       kT[:, dc, :].rearrange("p (b q) -> p b q", b=B),
                                                       halfmask[:, h:h + 1], None, ALU.mult)
                    last.then_inc(q_ready, 1)
                att_dve(dve, link, 1, False)

                ln_dve(dve, link, 2)
                xt_copy(dve, nc.vector.tensor_copy, 2, (1, 3))

                def shared_mul(k):
                    hf = k % 2
                    dve.wait_ge(sh_silu, k + 1)
                    dve.wait_ge(sh_u, k + 1)
                    if k >= 2:
                        dve.wait_ge(sh_t, k - 1)
                    nc.vector.tensor_tensor(shid[hf], sgate[hf], PS[:, 3 + 2 * hf, 0:I], ALU.mult).then_inc(sh_h, 1)

                def shared_add(t):
                    dve.wait_ge(sh_d, 2 * t + 2)
                    nc.vector.tensor_tensor(x[:, t, :], x[:, t, :], PS[:, 7, :], ALU.add).then_inc(sh_y, 1)

                fl = lambda v: v.rearrange("p a b -> p (a b)")
                dve.wait_ge(lg_exp, 1)
                dve.wait_ge(ld_gate, 32)
                dve.wait_ge(zpad_set, 1)
                link(nc.vector.tensor_scalar(fl(scores), fl(scores), 1.0, None, ALU.add))
                link(nc.vector.reciprocal(fl(scores), fl(scores)))
                link(nc.vector.tensor_tensor(choice, scores, gbias[:, :].unsqueeze(1).to_broadcast([P, NT, E]), ALU.add))
                for t in range(NT):
                    for g in range(NG):
                        last = nc.vector.max(srt[:, t, g, :], choice[:, t, 8 * g:8 * g + 8])
                link(last)
                link(nc.vector.tensor_tensor(gsum, srt[:, :, :, 0], srt[:, :, :, 1], ALU.add))
                for t in range(NT):
                    last = nc.vector.max(gtop[:, t, :], gsum[:, t, :])
                link(last)
                for t in range(NT):
                    last = nc.vector.max_index(gidx[:, t, :], gtop[:, t, :], gsum[:, t, :])
                link(last)
                shared_mul(0)
                shared_mul(1)
                link(nc.vector.tensor_copy(gidxf, gidx))
                link(nc.vector.tensor_tensor(
                    eqg, iota128[:, 0:NG].unsqueeze(1).unsqueeze(3).to_broadcast([P, NT, NG, TG]),
                    gidxf[:, :, 0:TG].unsqueeze(2).to_broadcast([P, NT, NG, TG]), ALU.is_equal))
                link(nc.vector.tensor_reduce(gmask.rearrange("p (a b) -> p a b", a=NT), eqg, AX.X, ALU.max))
                link(nc.vector.tensor_tensor(
                    tmp64.rearrange("p a (g k) -> p (a g) k", g=NG), choice.rearrange("p a (g k) -> p (a g) k", g=NG),
                    gmask.unsqueeze(2).to_broadcast([P, NT * NG, 8]), ALU.mult))
                for t in range(NT):
                    last = nc.vector.max(top8[:, t, :], tmp64[:, t, :])
                link(last)
                for t in range(NT):
                    last = nc.vector.max_index(idx8[:, t, :], top8[:, t, :], tmp64[:, t, :])
                link(last)
                link(nc.vector.tensor_copy(idx8f.rearrange("p (a b) -> p a b", a=NT), idx8))
                eqf, eqtf = (v.rearrange("p a b e -> p (a b) e") for v in (eq, eqt))
                link(nc.vector.tensor_tensor(eqf, iota128[:, 0:E].unsqueeze(1).to_broadcast([P, NT * 8, E]),
                                             idx8f.unsqueeze(2).to_broadcast([P, NT * 8, E]), ALU.is_equal))
                nc.vector.tensor_reduce(sel, eq.rearrange("p a k e -> p a e k"), AX.X, ALU.add).then_inc(sel_ready, 1)
                dve.wait_ge(sel_ready, 1)
                shared_mul(2)
                shared_mul(3)
                shared_add(0)
                link(nc.vector.tensor_tensor(tmp64, sel, scores, ALU.mult))
                link(nc.vector.tensor_reduce(wsum, tmp64, AX.X, ALU.add))
                link(nc.vector.tensor_scalar(wsum, wsum, 1e-20, None, ALU.add))
                link(nc.vector.reciprocal(wnorm, wsum))
                link(nc.vector.tensor_scalar(wnorm, wnorm, ROUTED_SCALE, None, ALU.mult))
                link(nc.vector.tensor_tensor(tmp64, tmp64, wnorm.unsqueeze(2).to_broadcast([P, NT, E]), ALU.mult))
                link(nc.vector.tensor_tensor(eqt, eq, tmp64.unsqueeze(2).to_broadcast([P, NT, 8, E]), ALU.mult))
                link(nc.vector.tensor_reduce(wk, eqtf, AX.X, ALU.add))
                dve.wait_ge(rank_made, 1)
                link(nc.vector.tensor_copy(cnt, PS[:, 0, NT * E:(NT + 1) * E]))
                link(nc.vector.tensor_scalar(ntile, cnt, 0.0, None, ALU.is_gt))
                for j in range(1, T // P):
                    link(nc.vector.scalar_tensor_tensor(out=ntile, in0=cnt, scalar=float(j * P), in1=ntile,
                                                        op0=ALU.is_gt, op1=ALU.add))
                link(nc.vector.memset(base, 0.0))
                link(nc.vector.tensor_tensor_scan(cum, ntile, base, 0.0, ALU.add, ALU.add))
                link(nc.vector.tensor_tensor(base, cum, ntile, ALU.subtract))
                link(nc.vector.tensor_scalar(base, base, float(P), None, ALU.mult))
                link(nc.vector.tensor_tensor(slotm, PS[:, 0, 0:NT * E].rearrange("p (a b) -> p a b", a=NT),
                                             base.unsqueeze(1).to_broadcast([P, NT, E]), ALU.add))
                link(nc.vector.tensor_scalar(cmp64, cum, iotap[:, 0:1], None, ALU.is_le))
                link(nc.vector.tensor_reduce(eot[:, 0:1], cmp64, AX.X, ALU.add))
                nc.vector.tensor_scalar(eot[:, 0:1], eot[:, 0:1], float(E - 1), None, ALU.min).then_inc(eot_ready, 1)
                shared_mul(4)
                shared_mul(5)
                shared_add(1)
                link(nc.vector.tensor_tensor(eqt, eq, slotm.unsqueeze(2).to_broadcast([P, NT, 8, E]), ALU.mult))
                link(nc.vector.tensor_reduce(slk, eqtf, AX.X, ALU.add))
                link(nc.vector.tensor_scalar(sdiv, slk, 1.0 / P, -63.5 / P, ALU.mult, ALU.add))
                link(nc.vector.tensor_scalar(sdiv, sdiv, ROUND, None, ALU.add))
                link(nc.vector.tensor_scalar(sdiv, sdiv, -ROUND, None, ALU.add))
                link(nc.vector.scalar_tensor_tensor(out=smod, in0=sdiv, scalar=-float(P), in1=slk,
                                                    op0=ALU.mult, op1=ALU.add))
                link(nc.vector.tensor_tensor(tokv.rearrange("p (a b) -> p a b", a=NT),
                                             tok_id[:, :].unsqueeze(2).to_broadcast([P, NT, 8]),
                                             smod.rearrange("p (a b) -> p a b", a=NT), ALU.subtract))
                shared_mul(6)
                shared_add(2)
                shared_mul(7)
                for t in range(NT):
                    k8 = slice(8 * t, 8 * t + 8)
                    if t >= 2:
                        dve.wait_ge(tab_made, t - 1)
                    if t >= 1:
                        dve.wait_ge(ab_ready, t)
                    nc.vector.tensor_tensor(oneA[t % 2], iota128.unsqueeze(1).to_broadcast([P, 8, P]),
                                            smod[:, k8].unsqueeze(2).to_broadcast([P, 8, P]), ALU.is_equal)
                    link(nc.vector.tensor_tensor(eqB, iota128[:, 0:NCOL].unsqueeze(1).to_broadcast([P, 8, NCOL]),
                                                 sdiv[:, k8].unsqueeze(2).to_broadcast([P, 8, NCOL]), ALU.is_equal))
                    nc.vector.tensor_tensor(twoB[t % 2][:, :, 0, :], eqB,
                                            tokv[:, k8].unsqueeze(2).to_broadcast([P, 8, NCOL]), ALU.mult)
                    nc.vector.tensor_tensor(twoB[t % 2][:, :, 1, :], eqB,
                                            wk[:, k8].unsqueeze(2).to_broadcast([P, 8, NCOL]),
                                            ALU.mult).then_inc(ab_ready, 1)
                dve.wait_ge(eot_made, 1)
                nc.vector.tensor_copy(eot_row[:, :], PS[0:1, 0, 0:P])
                link(nc.vector.tensor_scalar(wsum[:, 0:1], cum[:, E - 1:E], 0.5, 0.25, ALU.mult, ALU.add))
                link(nc.vector.tensor_scalar(wsum[:, 0:1], wsum[:, 0:1], ROUND, None, ALU.add))
                link(nc.vector.tensor_scalar(wsum[:, 0:1], wsum[:, 0:1], -ROUND - 2.0, None, ALU.add))
                nc.vector.tensor_copy(n_iter[:, :], wsum[0:1, 0:1])
                dve.wait_ge(tab_made, NT)
                nc.vector.tensor_scalar(idx_tab[:, :], PS[:, 1, 0:NCOL], pad_row[:, 0:1], None, ALU.add)
                nc.vector.tensor_copy(w_tab[:, :], PS[:, 1, NCOL:2 * NCOL]).then_inc(tables, 1)
                shared_add(3)
                dve.wait_ge(tables, 1)
                dve.wait_ge(sh_y, NT)

        def iterations(eng):
            return eng.value_load(n_iter[0:1, 0:1], min_val=14, max_val=(MAXT + 1) // 2 - 2) + 2

        with nc.Block() as block:
            @block.sync
            def _(sp):
                def load(r, k, col):
                    i = 2 * r + k
                    e = sp.value_load(eot_row[0:1, col], min_val=0, max_val=E - 1)
                    ev = bass.ds(e, 1)
                    if r is not first:
                        sp.wait_ge(u_made, i - 1)
                    sp.dma_start(wgu[k].rearrange("p c g i -> p (c g i)"),
                                 a["w_gu2"][ev, :, :].rearrange("e p n -> (e p) n")).then_inc(w_gu[k], 16)
                    if r is not first:
                        sp.wait_ge(y_made, i - 1)
                    sp.dma_start(wdn[k][:, 0:2, :].rearrange("p c n -> p (c n)"),
                                 a["w_dna2"][ev, :, :].rearrange("e p n -> (e p) n")).then_inc(w_dn[k], 16)
                    sp.dma_start(wdn[k][0:96, 2, :],
                                 a["w_dnb"][ev, :, :].rearrange("e p n -> (e p) n")).then_inc(w_dn[k], 16)

                first = 0
                n = iterations(sp)
                load(first, 0, slice(0, 1))
                load(first, 1, slice(1, 2))
                sp.dma_start(wkv, a["l1_wkv"]).then_inc(ld_wkv, 16)
                for c, (k0, w) in enumerate(KC):
                    sp.dma_start(ctxT[:, :, k0:k0 + w], a["ctxT"][0, :, :, k0:k0 + w]).then_inc(ctx_ld[c], 16)
                sp.dma_start(mask8[:, :], a["mask"][0:1, :].to_broadcast([P, S2])).then_inc(mask_ld, 16)
                sp.dma_start(vbias[:, :], a["l1_bv"].to_broadcast([P, D])).then_inc(ld_vb1, 16)
                with sp.Fori(1, n) as r:
                    for k in range(2):
                        load(r, k, bass.ds(2 * r + k, 1))
                sp.wait_ge(y_added, 32 * n)
                sp.dma_start(x[:, :, :], acc[0:T, :].rearrange("(t p) d -> p t d", p=P)).then_inc(acc_in, 16)
                sp.wait_ge(acc_in, 16)

            @block.gpsimd
            def _(pool):
                def gather(r, k, col):
                    i = 2 * r + k
                    pool.wait_ge(tables, 1)
                    if r is not first:
                        pool.wait_ge(xg_made, i - 1)
                    if r is not first or k == 1:
                        pool.wait_ge(xg_loaded[1 - k], 16 * (r + k))
                    nc.gpsimd.tensor_copy(gcol[:, :], idx_tab[:, col]).then_inc(gcol_set, 1)
                    col_set = count(pool, i + 1)
                    pool.wait_ge(tables, 1)
                    pool.wait_ge(gcol_set, col_set)
                    pool.indirect_dma_start(out=xg[k], out_offset=None, in_=xrow,
                                            in_offset=bass.IndirectOffsetOnAxis(ap=gcol[:, 0:1], axis=0)
                                            ).then_inc(xg_loaded[k], 16)

                def scatter(r, k, col):
                    i = 2 * r + k
                    pool.wait_ge(tables, 1)
                    pool.wait_ge(y_ready, i + 1)
                    pool.wait_ge(y_added, 16 * i)
                    nc.gpsimd.tensor_copy(scol[:, :], idx_tab[:, col]).then_inc(scol_set, 1)
                    col_set = count(pool, i + 1)
                    pool.wait_ge(tables, 1)
                    pool.wait_ge(scol_set, col_set)
                    pool.indirect_dma_start(out=acc, out_offset=bass.IndirectOffsetOnAxis(ap=scol[:, 0:1], axis=0),
                                            in_=yrow[k], in_offset=None, compute_op=ALU.add).then_inc(y_added, 16)

                first = 0
                n = iterations(pool)
                gather(first, 0, slice(0, 1))
                gather(first, 1, slice(1, 2))
                with pool.Fori(1, n) as r:
                    for k in range(2):
                        gather(r, k, bass.ds(2 * r + k, 1))
                        scatter(r - 1, k, bass.ds(2 * r + k - 2, 1))
                for k in range(2):
                    scatter(n - 1, k, bass.ds(2 * n + k - 2, 1))

            @block.tensor
            def _(pe):
                def rows_t(r, k):
                    pe.wait_ge(xg_loaded[k], 16 * (r + 1))
                    if r is not first or k == 1:
                        pe.wait_ge(xg_ready, 2 * r + k)
                    for c in range(NC):
                        last = nc.tensor.transpose(PS[:, 4, c * P:(c + 1) * P], xg[k][:, c * P:(c + 1) * P], ident[:, :])
                    last.then_inc(xg_made, 1)

                def gate_up(r, k, gu):
                    i = 2 * r + k
                    if gu == 0:
                        pe.wait_ge(xg_ready, i + 1)
                        pe.wait_ge(w_gu[k], 16 * (r + 1))
                    if r is not first or k == 1:
                        pe.wait_ge(h_ready if gu else silu_ready, i)
                    for c in range(NC):
                        last = nc.tensor.matmul(PS[:, gu, 0:I], xgT[k][:, c, :], wgu[k][:, c, gu, :],
                                                start=(c == 0), stop=(c == NC - 1))
                    last.then_inc(u_made if gu else g_made, 1)

                def hidden_t(r, k):
                    i = 2 * r + k
                    pe.wait_ge(h_ready, i + 1)
                    if r is not first or k == 1:
                        pe.wait_ge(ht_ready, i)
                    for j, (i0, w) in enumerate(IJ):
                        last = nc.tensor.transpose(PS[0:w, 2, j * P:(j + 1) * P], hid[:, i0:i0 + w], ident[:, :])
                    last.then_inc(ht_made, 1)

                def down(r, k):
                    i = 2 * r + k
                    pe.wait_ge(ht_ready, i + 1)
                    pe.wait_ge(w_dn[k], 32 * (r + 1))
                    if r is not first or k == 1:
                        pe.wait_ge(y_ready, i)
                    for j, (i0, w) in enumerate(IJ):
                        last = nc.tensor.matmul(PS[:, 3, :], hT[0:w, j, :], wdn[k][0:w, j, :],
                                                start=(j == 0), stop=(j == 2))
                    last.then_inc(y_made, 1)

                first = 0
                n = iterations(pe)
                pe.wait_ge(tables, 1)

                def turn(r, k, before, more=True):
                    gate_up(r, k, 0)
                    if before is not None:
                        hidden_t(before, 1 - k)
                    if more:
                        rows_t(r + k, 1 - k)
                    gate_up(r, k, 1)
                    if before is not None:
                        down(before, 1 - k)

                rows_t(first, 0)
                turn(first, 0, None)
                turn(first, 1, first)
                with pe.Fori(1, n - 1) as r:
                    turn(r, 0, r - 1)
                    turn(r, 1, r)
                turn(n - 1, 0, n - 2)
                turn(n - 1, 1, n - 1, more=False)
                hidden_t(n - 1, 1)
                down(n - 1, 1)

            @block.scalar
            def _(act):
                def rows_copy(r, k):
                    act.wait_ge(xg_made, 2 * r + k + 1)
                    nc.scalar.copy(xgT[k].rearrange("p a b -> p (a b)"), PS[:, 4, :]).then_inc(xg_ready, 1)

                def silu(r, k):
                    i = 2 * r + k
                    act.wait_ge(g_made, i + 1)
                    if r is not first or k == 1:
                        act.wait_ge(h_ready, i)
                    nc.scalar.activation(act_g, PS[:, 0, 0:I], ACT.Silu).then_inc(silu_ready, 1)

                def rows_out_copy(r, k, col):
                    i = 2 * r + k
                    act.wait_ge(y_made, i + 1)
                    if r is not first:
                        act.wait_ge(y_added, 16 * (i - 1))
                    nc.scalar.activation(yrow[k], PS[:, 3, :], ACT.Copy, scale=w_tab[:, col]).then_inc(y_ready, 1)

                def turn(r, k, before, col, more=True):
                    silu(r, k)
                    if more:
                        rows_copy(r + k, 1 - k)
                    if before is not None:
                        rows_out_copy(before, 1 - k, col)

                first = 0
                n = iterations(act)
                act.wait_ge(tables, 1)
                rows_copy(first, 0)
                turn(first, 0, None, None)
                turn(first, 1, first, slice(0, 1))
                turn(1, 0, first, slice(1, 2))
                turn(1, 1, 1, slice(2, 3))
                with act.Fori(2, n - 1) as r:
                    turn(r, 0, r - 1, bass.ds(2 * r - 1, 1))
                    turn(r, 1, r, bass.ds(2 * r, 1))
                turn(n - 1, 0, n - 2, bass.ds(2 * n - 3, 1))
                turn(n - 1, 1, n - 1, bass.ds(2 * n - 2, 1), more=False)
                rows_out_copy(n - 1, 1, bass.ds(2 * n - 1, 1))

            @block.vector
            def _(dve):
                def mul(r, k):
                    i = 2 * r + k
                    dve.wait_ge(silu_ready, i + 1)
                    dve.wait_ge(u_made, i + 1)
                    if r is not first or k == 1:
                        dve.wait_ge(ht_made, i)
                    nc.vector.tensor_tensor(hid, act_g, PS[:, 1, 0:I], ALU.mult).then_inc(h_ready, 1)

                def hidden_copy(r, k):
                    i = 2 * r + k
                    dve.wait_ge(ht_made, i + 1)
                    if r is not first or k == 1:
                        dve.wait_ge(y_made, i)
                    nc.vector.tensor_copy(hT[:, 0:2, :], PS[:, 2, 0:2 * P].rearrange("p (a b) -> p a b", a=2))
                    nc.vector.tensor_copy(hT[0:96, 2, :], PS[0:96, 2, 2 * P:3 * P]).then_inc(ht_ready, 1)

                first = 0
                n = iterations(dve)
                dve.wait_ge(tables, 1)
                mul(first, 0)
                hidden_copy(first, 0)
                mul(first, 1)
                with dve.Fori(1, n) as r:
                    hidden_copy(r - 1, 1)
                    mul(r, 0)
                    hidden_copy(r, 0)
                    mul(r, 1)
                hidden_copy(n - 1, 1)

        GROUPS = []
        for c in range(4):
            GROUPS += [("k", 0, c), ("k", 1, c)]
            GROUPS += [("v", kt, c) for kt in range(KT_N) if kt // 4 == c]
        NGR = len(GROUPS)
        NK = [sum(1 for q in GROUPS[:g] if q[0] == "k") for g in range(NGR + 1)]
        NV = [sum(1 for q in GROUPS[:g] if q[0] == "v") for g in range(NGR + 1)]
        SHARE = [([0, 1, 2], [3], [4], [5]), ([6, 7], [8], [9], [10]),
                 ([11, 12], [13], [14], [15]), ([16, 17], [18], [19], [20])]
        KTS = [[kt for kt in range(KT_N) if kt // 4 == tg] for tg in range(4)]
        rows = lambda kt: min(P, S2 - kt * P)
        half_of = lambda hf, g: 6 + (NGR * hf + g) % 2

        with nc.Block() as block:
            @block.sync
            def _(sp):
                sp.dma_start(bias_r[:, :], a["l1_bo"].to_broadcast([P, D])).then_inc(ld_bo1, 16)

                def load_ctx(b, bv):
                    for c, (k0, n) in enumerate(KC):
                        sp.wait_ge(vx_made, KT_N * (2 * b - 1) + NV[NGR] * 0 + sum(len(q) for q in KTS[:c + 1]))
                        sp.dma_start(ctxT[:, :, k0:k0 + n],
                                     a["ctxT"][bv, :, :, k0:k0 + n].rearrange("e p c k -> (e p) c k")
                                     ).then_inc(ctx_ld[c], 16)

                sp.wait_ge(mask_set, 1)
                sp.dma_start(mask8[:, :], a["mask"][1:2, :].to_broadcast([P, S2])).then_inc(mask_ld, 16)
                load_ctx(1, slice(1, 2))
                sp.wait_ge(q_made, 2 * NC + NC)
                sp.dma_start(slot[0][:, :, :], a["l1a_wk"]).then_inc(ld_l1a, 16)
                with sp.Fori(2, B) as b:
                    sp.wait_ge(ld_l1q, 16)
                    sp.wait_ge(mask_set, b)
                    sp.dma_start(mask8[:, :], a["mask"][bass.ds(b, 1), :].to_broadcast([P, S2])).then_inc(mask_ld, 16)
                    load_ctx(b, bass.ds(b, 1))
                sp.wait_ge(xb_ready, 3)
                sp.wait_ge(xx_ready, NT)
                sp.dma_start(bias_r[:, :], a["l1a_bo"].to_broadcast([P, D])).then_inc(ld_boa1, 16)
                sp.dma_start(slot[2][:, :, :], a["l1a_wo"]).then_inc(ld_l1ao, 16)

            @block.gpsimd
            def _(pool):
                ln_pool(pool, 3)
                pool.wait_ge(ld_bo1, 16)
                add_out_bias(pool, 2, 4)

                def take_q(b, hf, bv):
                    nc.gpsimd.tensor_copy(qbh[hf][:, :, :].unsqueeze(2), qbd[:, 2 * hf:2 * hf + 2, bv, :]
                                          ).then_inc(qh_ready, 1)

                pool.wait_ge(q_ready, 3 * NC)
                take_q(0, 0, slice(0, 1))
                take_q(0, 1, slice(0, 1))
                with pool.Fori(1, B) as b:
                    for hf in range(2):
                        pool.wait_ge(q_ready, 3 * NC)
                        pool.wait_ge(sx_made, 32 * b + 16 * hf - 16)
                        take_q(b, hf, bass.ds(b, 1))

            @block.tensor
            def _(pe):
                def group(b, hf, g):
                    kind, i, c = GROUPS[g]
                    u = 2 * b + hf
                    bank = half_of(hf, g)
                    if hf == 0 and (g == 0 or GROUPS[g - 1][2] != c):
                        pe.wait_ge(ctx_ld[c], 16 * (b + 1))
                    if g >= 2 or not (isinstance(b, int) and b == 0 and hf == 0):
                        g2, u2 = (g - 2, u) if g >= 2 else (NGR + g - 2, u - 1)
                        if GROUPS[g2][0] == "k":
                            pe.wait_ge(kx_ready, 8 * u2 + NK[g2 + 1])
                        else:
                            pe.wait_ge(vx_ready, KT_N * u2 + NV[g2 + 1])
                    if kind == "k":
                        k0, n = KC[c]
                        f0 = (2 * hf + i) * P
                        for cc in range(NC):
                            last = nc.tensor.matmul(PS[:, bank, 0:n], wkv[:, cc, f0:f0 + P], ctxT[:, cc, k0:k0 + n],
                                                    start=(cc == 0), stop=(cc == NC - 1))
                        last.then_inc(kx_made, 1)
                    else:
                        n, f0 = rows(i), D + hf * 256
                        for cc in range(NC):
                            last = nc.tensor.matmul(PS[0:n, bank, 0:256], ctxT[:, cc, i * P:i * P + n],
                                                    wkv[:, cc, f0:f0 + 256], start=(cc == 0), stop=(cc == NC - 1))
                        last.then_inc(vx_made, 1)

                def score(b, hf, j, c):
                    u, r, (k0, n) = 2 * b + hf, 64 * (j % 2), KC[c]
                    if j == 0 and c == 0:
                        pe.wait_ge(qh_ready, u + 1)
                        pe.wait_ge(kx_ready, 8 * (u + 1))
                    if c >= 2:
                        pe.wait_ge(sx_read, 16 * u + 4 * j + c - 1)
                    nc.tensor.matmul(PS[:, c % 2, 0:n], qbh[hf][r:r + 64, j // 2, :],
                                     kTx[hf][r:r + 64, j // 2, k0:k0 + n], start=True, stop=True).then_inc(sx_made, 1)

                def turn_p(u, j, tg):
                    if tg == 0:
                        pe.wait_ge(px_ready, 4 * u + j + 1)
                    for i, kt in enumerate(KTS[tg]):
                        n = rows(kt)
                        last = nc.tensor.transpose(PS[0:n, 2 + tg % 2, i * P:(i + 1) * P],
                                                   sx[j % 2][:, kt * P:kt * P + n], ident[:, :])
                    last.then_inc(ptx_made, 1)

                def pv(u, hf, j, tg):
                    pe.wait_ge(ptx_dve if tg % 2 else ptx_act, 8 * u + 2 * j + tg // 2 + 1)
                    if tg == 0:
                        pe.wait_ge(zx_ready, 4 * u + j)
                        if j == 0:
                            pe.wait_ge(vx_ready, KT_N * (u + 1))
                    for i, kt in enumerate(KTS[tg]):
                        n = rows(kt)
                        last = nc.tensor.matmul(PS[:, 4, 0:64], pTx[tg % 2][0:n, i, :],
                                                vx[hf][0:n, kt, j * 64:(j + 1) * 64],
                                                start=(kt == 0), stop=(kt == KT_N - 1))
                    last.then_inc(pvx_part, 1)

                def unit(b, hf, nxt):
                    u = 2 * b + hf
                    for j in range(4):
                        share = SHARE[j] if nxt is not None else ([], [], [], [])
                        for g in share[0]:
                            group(*nxt, g)
                        turn_p(u, j, 0)
                        turn_p(u, j, 1)
                        for g in share[1]:
                            group(*nxt, g)
                        pv(u, hf, j, 0)
                        pv(u, hf, j, 1)
                        turn_p(u, j, 2)
                        turn_p(u, j, 3)
                        for g in share[2]:
                            group(*nxt, g)
                        pv(u, hf, j, 2)
                        pv(u, hf, j, 3)
                        ahead = (b, hf, j + 1) if j < 3 else (None if nxt is None else (*nxt, 0))
                        if ahead:
                            score(*ahead, 0)
                            score(*ahead, 1)
                        if j == 3:
                            pe.wait_ge(zx_ready, 4 * u + 4)
                            pe.wait_ge(ztx_ready, u)
                            nc.tensor.transpose(PS[:, 5, 0:P], z[:, hf, 0:4, :].rearrange("p a b -> p (a b)"),
                                                ident[:, :]).then_inc(ztx_made, 1)
                        for g in share[3]:
                            group(*nxt, g)
                        if ahead:
                            score(*ahead, 2)
                            score(*ahead, 3)

                xt_pe(pe, 3)
                pe.wait_ge(ld_l1q, 16)
                q_pe(pe, slot[0], 3, 2)
                pe.wait_ge(q_ready, 3 * NC)
                pe.wait_ge(ld_wkv, 16)
                for g in range(NGR):
                    group(0, 0, g)
                for c in range(4):
                    score(0, 0, 0, c)
                with pe.Fori(0, B - 1) as b:
                    unit(b, 0, (b, 1))
                    unit(b, 1, (b + 1, 0))
                unit(B - 1, 0, (B - 1, 1))
                unit(B - 1, 1, None)
                pe.wait_ge(ztx_ready, 2 * B)
                pe.wait_ge(ld_l1o, 16)
                for t in range(NT):
                    for jh in range(4):
                        last = nc.tensor.matmul(PS[:, t, :], zT[:, jh // 2, jh % 2, t * P:(t + 1) * P],
                                                slot[2][:, jh, :], start=(jh == 0), stop=(jh == 3))
                    last.then_inc(pj1_made, 1)

            @block.scalar
            def _(act):
                def k_out(b, hf, g):
                    kind, i, c = GROUPS[g]
                    if kind == "k":
                        k0, n = KC[c]
                        act.wait_ge(kx_made, 8 * (2 * b + hf) + NK[g + 1])
                        nc.scalar.activation(kTx[hf][:, i, k0:k0 + n], PS[:, half_of(hf, g), 0:n], ACT.Identity,
                                             bias=bias_c[:, 3, 2 * hf + i:2 * hf + i + 1]).then_inc(kx_ready, 1)

                def ex(u, j):
                    act.wait_ge(sx_max, 4 * u + j + 1)
                    nc.scalar.activation(sx[j % 2][:, 0:S2], sx[j % 2][:, 0:S2], ACT.Exp, scale=SC,
                                         bias=nmx[:, j % 2:j % 2 + 1],
                                         accum_out=rsx[:, j % 2:j % 2 + 1]).then_inc(px_ready, 1)

                def unit(b, hf, nxt, bv):
                    u = 2 * b + hf
                    for j in range(4):
                        share = SHARE[j] if nxt is not None else ([], [], [], [])
                        for g in share[0]:
                            k_out(*nxt, g)
                        for tg in (0, 2):
                            act.wait_ge(ptx_made, 16 * u + 4 * j + tg + 1)
                            nc.scalar.copy(pTx[0][:, :, :].rearrange("p a b -> p (a b)"),
                                           PS[:, 2, :]).then_inc(ptx_act, 1)
                            for g in share[1 + tg // 2]:
                                k_out(*nxt, g)
                        if j == 3:
                            act.wait_ge(ztx_made, u + 1)
                            nc.scalar.copy(zT[:, hf, :, bv],
                                           PS[:, 5, 0:P].rearrange("p (h q) -> p h q", h=2)).then_inc(ztx_ready, 1)
                        for g in share[3]:
                            k_out(*nxt, g)
                        if j < 3:
                            ex(u, j + 1)
                        elif nxt is not None:
                            ex(u + 1, 0)

                xt_copy(act, nc.scalar.copy, 3, (0, 2))
                for g in range(NGR):
                    k_out(0, 0, g)
                ex(0, 0)
                with act.Fori(0, B - 1) as b:
                    unit(b, 0, (b, 1), bass.ds(S1 * b, S1))
                    unit(b, 1, (b + 1, 0), bass.ds(S1 * b, S1))
                unit(B - 1, 0, (B - 1, 1), slice(T - S1, T))
                unit(B - 1, 1, None, slice(T - S1, T))

            @block.vector
            def _(dve):
                link = Chain(dve, dve_seq3)
                seq = dve_x

                def v_out(b, hf, g):
                    kind, i, c = GROUPS[g]
                    if kind == "v":
                        n = rows(i)
                        dve.wait_ge(vx_made, KT_N * (2 * b + hf) + NV[g + 1])
                        nc.vector.tensor_tensor(vx[hf][0:n, i, :], PS[0:n, half_of(hf, g), 0:256],
                                                vbias[0:n, hf * 256:hf * 256 + 256], ALU.add).then_inc(vx_ready, 1)

                def masked(u, j, c):
                    k0, n = KC[c]
                    made = count(dve, 16 * u + 4 * j + c + 1)
                    dve.wait_ge(ld_vb1, 16)
                    dve.wait_ge(sx_made, made)
                    nc.vector.tensor_tensor_reduce(out=sx[j % 2][:, k0:k0 + n], in0=PS[:, c % 2, 0:n],
                                                   in1=maskadd[:, k0:k0 + n], scale=1.0, scalar=-3e38, op0=ALU.add,
                                                   op1=ALU.max, accum_out=mx4[:, c:c + 1]).then_inc(sx_read, 1)

                def row_max(u, j):
                    n = 4 * u + j
                    dve.wait_ge(sx_read, 4 * n + 4)
                    nc.vector.tensor_reduce(nmx[:, j % 2:j % 2 + 1], mx4[:, :], AX.X, ALU.max).then_inc(seq, 1)
                    dve.wait_ge(seq, n + 1)
                    nc.vector.tensor_scalar(nmx[:, j % 2:j % 2 + 1], nmx[:, j % 2:j % 2 + 1], -SC, None,
                                            ALU.mult).then_inc(sx_max, 1)

                def set_mask(count):
                    dve.wait_ge(mask_ld, 16 * count)
                    nc.vector.tensor_scalar(maskadd[:, :], mask8[:, :], NEG, None, ALU.mult).then_inc(mask_set, 1)
                    dve.wait_ge(mask_set, count)

                def unit(b, hf, nxt, last=False):
                    u = 2 * b + hf
                    for j in range(4):
                        share = SHARE[j] if nxt is not None else ([], [], [], [])
                        for g in share[0]:
                            v_out(*nxt, g)
                        dve.wait_ge(px_ready, 4 * u + j + 1)
                        nc.vector.reciprocal(rix[:, j % 2:j % 2 + 1], rsx[:, j % 2:j % 2 + 1]).then_inc(rix_ready, 1)
                        for tg in (1, 3):
                            dve.wait_ge(ptx_made, 16 * u + 4 * j + tg + 1)
                            n = rows(KTS[tg][0]) if tg == 3 else P
                            w = len(KTS[tg]) * P
                            nc.vector.tensor_copy(pTx[1][0:n, :, :].rearrange("p a b -> p (a b)")[:, 0:w],
                                                  PS[0:n, 3, 0:w]).then_inc(ptx_dve, 1)
                            for g in share[1 + tg // 2]:
                                v_out(*nxt, g)
                        dve.wait_ge(rix_ready, 4 * u + j + 1)
                        dve.wait_ge(pvx_part, 16 * u + 4 * j + 4)
                        for h in range(2):
                            r = slice(64 * h, 64 * h + 64)
                            ins = nc.vector.tensor_scalar(z[r, hf, j, :], PS[r, 4, h * HD:(h + 1) * HD],
                                                          rix[r, j % 2:j % 2 + 1], None, ALU.mult)
                        ins.then_inc(zx_ready, 1)
                        if hf == 1 and j == 3 and nxt is not None:
                            set_mask(b + 2)
                        ahead = (u, j + 1) if j < 3 else (None if nxt is None else (u + 1, 0))
                        if ahead:
                            masked(*ahead, 0)
                            masked(*ahead, 1)
                        for g in share[3]:
                            v_out(*nxt, g)
                        if ahead:
                            masked(*ahead, 2)
                            masked(*ahead, 3)
                            row_max(*ahead)

                ln_dve(dve, link, 3)
                xt_copy(dve, nc.vector.tensor_copy, 3, (1, 3))
                q_dve(dve, 2, 2)
                set_mask(1)
                dve.wait_ge(ld_wkv, 16)
                dve.wait_ge(ld_vb1, 16)
                for g in range(NGR):
                    v_out(0, 0, g)
                for c in range(4):
                    masked(0, 0, c)
                row_max(0, 0)
                with dve.Fori(0, B - 1) as b:
                    unit(b, 0, (b, 1))
                    unit(b, 1, (b + 1, 0))
                unit(B - 1, 0, (B - 1, 1))
                unit(B - 1, 1, None)
                dve.wait_ge(xb_ready, 3)
                for t in range(NT):
                    dve.wait_ge(pj1_made, t + 1)
                    nc.vector.tensor_tensor(x[:, t, :], x[:, t, :], PS[:, t, :], ALU.add).then_inc(xx_ready, 1)
                dve.wait_ge(xx_ready, NT)

        with nc.Block() as block:
            @block.sync
            def _(sp):
                sp.dma_start(rhs, a["l1_rhs"]).then_inc(ld_rhs, 16)
                for t in range(NT):
                    sp.wait_ge(ff_x, t + 1)
                    sp.dma_start(out[t * P:(t + 1) * P, :], x[:, t, :]).then_inc(out_done, 16)
                sp.wait_ge(out_done, 16 * NT)

            @block.gpsimd
            def _(pool):
                link = Chain(pool, pool_seq4)
                ln_pool(pool, 4)
                pool.wait_ge(ld_boa1, 16)
                add_out_bias(pool, 3, 5)
                pool.wait_ge(rabs_ready, 1)
                nc.gpsimd.partition_all_reduce(rscale, rabs, P, RMAX).then_inc(rmax_ready, 1)
                ln_pool(pool, 5)

            @block.tensor
            def _(pe):
                xt_pe(pe, 4)
                pe.wait_ge(ld_l1a, 48)
                q_pe(pe, slot[3], 4, 3)
                for dc in range(NC):
                    for c in range(NC):
                        last = nc.tensor.matmul(PS[:, dc, :], slot[0][:, c, dc * P:(dc + 1) * P], xnT[:, c, :],
                                                start=(c == 0), stop=(c == NC - 1))
                    last.then_inc(k_made, 1)
                pe.wait_ge(q_ready, 4 * NC)
                for t in range(NT):
                    for c in range(NC):
                        last = nc.tensor.matmul(PS[:, 4 + t, :], xnT[:, c, t * P:(t + 1) * P], slot[1][:, c, :],
                                                start=(c == 0), stop=(c == NC - 1))
                    last.then_inc(v_made, 1)
                pe.wait_ge(k_ready, 3 * NC)
                pe.wait_ge(v_ready, 3 * NT)
                pe.wait_ge(ld_l1ao, 16)
                att_pe(pe, 2, slot[2])
                for t in range(NT):
                    pe.wait_ge(lq_made, t + 1)
                    for c in range(NC):
                        last = nc.tensor.transpose(PS[:, t, c * P:(c + 1) * P], xn[:, t, c * P:(c + 1) * P], ident[:, :])
                    last.then_inc(xt_made, 1)
                pe.wait_ge(rq_ready, 1)
                for t in range(NT):
                    pe.wait_ge(lq_ready, t + 1)
                    for c in range(NC):
                        last = nc.tensor.matmul(PS[:, 4 + t, :], lq[:, c, t * P:(t + 1) * P], rq[:, c, :],
                                                start=(c == 0), stop=(c == NC - 1))
                    last.then_inc(ff_made, 1)

            @block.scalar
            def _(act):
                xt_copy(act, nc.scalar.copy, 4, (0, 2))
                for dc in range(NC):
                    act.wait_ge(k_made, NC + dc + 1)
                    nc.scalar.copy(kT[:, dc, :], PS[:, dc, :]).then_inc(k_ready, 1)
                for t in range(NT):
                    act.wait_ge(v_made, 2 * NT + t + 1)
                    nc.scalar.copy(v64[:, t, :], PS[:, 4 + t, :]).then_inc(v_ready, 1)
                att_act(act, 2, SC)
                for t in range(NT):
                    act.wait_ge(xt_made, 5 * NT + t + 1)
                    nc.scalar.copy(lq[:, :, t * P:(t + 1) * P],
                                   PS[:, t, :].rearrange("p (c k) -> p c k", c=NC)).then_inc(lq_ready, 1)

            @block.vector
            def _(dve):
                link = Chain(dve, dve_seq4)
                ln_dve(dve, link, 4)
                xt_copy(dve, nc.vector.tensor_copy, 4, (1, 3))
                q_dve(dve, 3, None)
                dve.wait_ge(ld_rhs, 16)
                nc.vector.tensor_reduce(rabs, rhs.rearrange("p c d -> p d c"), AX.X, ALU.max,
                                        apply_absolute_value=True).then_inc(rabs_ready, 1)
                att_dve(dve, link, 2, True)
                dve.wait_ge(rmax_ready, 1)
                link(nc.vector.tensor_scalar(rscale, rscale, 1e-12, 1.0 / 127.0, ALU.max, ALU.mult))
                link(nc.vector.reciprocal(rabs, rscale))
                link(nc.vector.tensor_tensor(rtmp, rhs, rabs.unsqueeze(1).to_broadcast([P, NC, D]), ALU.mult))
                link(nc.vector.tensor_scalar(rtmp, rtmp, ROUND, None, ALU.add))
                nc.vector.tensor_scalar(rq, rtmp, -ROUND, None, ALU.add).then_inc(rq_ready, 1)
                ln_dve(dve, link, 5)
                dve.wait_ge(xn_ready, 6 * NT)
                link(nc.vector.tensor_reduce(lscale, xn[:, :, :], AX.X, ALU.max, apply_absolute_value=True))
                link(nc.vector.tensor_scalar(lscale, lscale, 1e-12, 1.0 / 127.0, ALU.max, ALU.mult))
                link(nc.vector.reciprocal(linv, lscale))
                for t in range(NT):
                    last = nc.vector.tensor_scalar(xn[:, t, :], xn[:, t, :], linv[:, t:t + 1], ROUND,
                                                   ALU.mult, ALU.add)
                link(last)
                for t in range(NT):
                    nc.vector.tensor_scalar(xn[:, t, :], xn[:, t, :], -ROUND, None, ALU.add).then_inc(lq_made, 1)
                for t in range(NT):
                    dve.wait_ge(ff_made, t + 1)
                    nc.vector.scalar_tensor_tensor(out=rtmp[:, t, :], in0=PS[:, 4 + t, :], scalar=lscale[:, t:t + 1],
                                                   in1=rscale, op0=ALU.mult, op1=ALU.mult).then_inc(ff_y, 1)
                    dve.wait_ge(ff_y, t + 1)
                    nc.vector.tensor_tensor(x[:, t, :], x[:, t, :], rtmp[:, t, :], ALU.add).then_inc(ff_x, 1)


def _lin(w):
    return w.reshape(-1, P, w.shape[1]).transpose(1, 0, 2)


def _heads(w):
    return w.reshape(2, 4, 2, HD, w.shape[1]).transpose(1, 3, 0, 2, 4).reshape(P, 4, w.shape[1])


def _heads64(w):
    return w.reshape(4, 2, 2, HD, w.shape[1]).transpose(0, 3, 1, 2, 4).reshape(P, 4, w.shape[1])


def kernel(**inputs):
    import numpy as _np
    import concourse.bacc as _bacc
    from concourse.bass_utils import run_bass_kernel_spmd as _run

    g = {k: _np.asarray(v) for k, v in inputs.items()}
    col = lambda b: b.reshape(NC, P).T
    row = lambda b: b.reshape(1, -1)
    ctxT = g["ctx_1024"].transpose(0, 2, 1)
    gate = _np.concatenate([g["L0_ffn_Wg"], g["L0_ffn_Sg"].reshape(2, I, D)])
    up = _np.concatenate([g["L0_ffn_Wu"], g["L0_ffn_Su"].reshape(2, I, D)])
    down = _np.concatenate([g["L0_ffn_Wd"], g["L0_ffn_Sd"].reshape(D, 2, I).transpose(1, 0, 2)]).transpose(0, 2, 1)
    gu = _np.stack([gate, up], axis=1).reshape(NE, 2, I, NC, P).transpose(0, 4, 3, 1, 2)
    laid = {
        "x": g["x"].reshape(NT, P, D).transpose(1, 0, 2),
        "ctx0": ctxT[:, :, :S1].reshape(B, NC, P, S1).transpose(2, 1, 0, 3).reshape(P, NC, T),
        "ctxT": ctxT.reshape(B, NC, P, S2).transpose(0, 2, 1, 3),
        "mask": g["mask_BxS2_bk0"],
        "l0_wq": _lin(g["L0_xattn_wq"]), "l0_wk": _lin(g["L0_xattn_wk"]), "l0_wv": _lin(g["L0_xattn_wv"]),
        "l0_wo": _heads64(g["L0_xattn_wo"]),
        "l0_bv": row(g["L0_xattn_bv"]), "l0_bo": row(g["L0_xattn_bo"]),
        "bias_c": _np.stack([col(g["L0_xattn_bq"]), col(g["L0_xattn_bk"]), col(g["L1_xattn_bq"]),
                             col(g["L1_xattn_bkv"][:D])], axis=1),
        "l0a_wq": g["L0_attn_Wq"].reshape(NC, 4, HD, HD).transpose(1, 3, 0, 2).reshape(P, NC, HD),
        "l0a_wp": _heads64(g["L0_attn_Wp"].T), "l0a_bp": row(g["L0_attn_bp"]),
        "gate_w": _lin(g["L0_ffn_gate_w"].T), "gate_b": row(g["L0_ffn_gate_bias"]),
        "w_gu2": gu.reshape(NE, P, NC * 2 * I),
        "w_dna2": down[:, :2 * P].reshape(NE, 2, P, D).transpose(0, 2, 1, 3).reshape(NE, P, 2 * D),
        "w_dnb": down[:, 2 * P:],
        "l1_wq": _lin(g["L1_xattn_Wq"]), "l1_wkv": _lin(g["L1_xattn_Wkv"]), "l1_bv": row(g["L1_xattn_bkv"][D:]),
        "l1_wo": _heads(g["L1_xattn_Wo"]), "l1_bo": row(g["L1_xattn_bo"]),
        "l1a_wq": _lin(g["L1_attn_Wq"].T), "l1a_wk": _lin(g["L1_attn_Wk"].T), "l1a_wv": _lin(g["L1_attn_Wv"].T),
        "l1a_wo": _heads64(g["L1_attn_Wo"].T), "l1a_bo": row(g["L1_attn_bo"]),
        "l1_rhs": _lin(g["L1_ffn_rhs"]),
    }
    nc = _bacc.Bacc("TRN2", target_bir_lowering=False, num_devices=1)
    arrays, args = {}, {}
    for name, v in laid.items():
        v = _np.ascontiguousarray(v)
        arrays[f"in_{name}"] = v
        args[name] = nc.dram_tensor(f"in_{name}", v.shape, mybir.dt.from_np(v.dtype), kind="ExternalInput").ap()
    args["w_gu"] = args["w_gu2"].rearrange("e p (c g i) -> e p c g i", c=NC, g=2)
    args["w_dna"] = args["w_dna2"].rearrange("e p (c n) -> e p c n", c=2)
    y = nc.dram_tensor("out_0", (T, D), F32, kind="ExternalOutput").ap()
    perceiver(nc, args, y)
    r = _run(nc, [arrays], core_ids=[0])
    return r.results[0]["out_0"].reshape(B, S1, D)
```

```python
from contextlib import ExitStack

import numpy as np
import concourse.bass as bass
from concourse import mybir

F32 = mybir.dt.float32
F32R = mybir.dt.float32r
BF16 = mybir.dt.bfloat16
I32 = mybir.dt.int32
U32 = mybir.dt.uint32
U8 = mybir.dt.uint8
ALU = mybir.AluOpType
ACT = mybir.ActivationFunctionType
AX = mybir.AxisListType
RMAX = bass.bass_isa.ReduceOp.max

P = 128
B, S1, D, S2 = 8, 64, 512, 1601
T = B * S1
NT = T // P
NC = D // P
H, HD = 16, 32
NP = H // 2
E, I, TOPK, NG, TG = 64, 352, 8, 8, 4
NE = E + 2
MAXT = (T * TOPK + E * (P - 1)) // P
NBUF = 4
NCOL = -(-MAXT // NBUF) * NBUF
IJ = [(0, 128), (128, 128), (256, 96)]
KC = [(0, 512), (512, 512), (1024, 512), (1536, 65)]
KT_N = 13
SX_AT = 10752
EPS = 1e-5
NEG = -1e30
ROUND = 12582912.0
SC = float(HD) ** -0.5
ROUTED_SCALE = 2.5


def perceiver(nc, a, out):
    acc = nc.dram_tensor("moe_acc", (T + P, D), F32, kind="Internal").ap()
    xrow = nc.dram_tensor("moe_rows", (T + P, D), F32, kind="Internal").ap()

    with ExitStack() as ctx:
        def sb(name, shape, dt=F32):
            return ctx.enter_context(nc.sbuf_tensor(name, shape, dt))

        def sem(name):
            return ctx.enter_context(nc.semaphore(name))

        x = sb("x", [P, NT, D])
        xnT = sb("xnT", [P, NC, T])
        zT = xnT[:, :, :].rearrange("p (jj h) t -> p jj h t", jj=2)
        qbd = sb("qbd", [P, NC, B, P])
        z = sb("z", [P, 2, NP, HD])
        ident = sb("ident", [P, P])
        causal = sb("causal", [P, S1])
        halfmask = sb("halfmask", [P, 2])
        bias_c = sb("bias_c", [P, 4, NC])
        bias_r = sb("bias_r", [P, D])
        vbias = sb("vbias", [P, D])
        gbias = sb("gbias", [P, E])
        wbd = sb("wbd", [P, NC, P])
        wsmall = sb("wsmall", [P, NC, HD])
        gatew = sb("gatew", [P, NC, E])
        st = sb("st", [P, NT, 6])
        mv = sb("mv", [P, NT, 2])
        rstd = sb("rstd", [P, NT])
        neg_half = sb("neg_half", [P, NT])
        smx = sb("smx", [P, 2, 16])
        ssum = sb("ssum", [P, 16])
        rinv = sb("rinv", [P, 16])
        mask8 = sb("mask8", [P, S2], U8)
        maskadd = sb("maskadd", [P, S2], BF16)
        R0 = sb("R0", [P, 13400])
        S_N = 14200 + NT * D + 4 * NC * D
        with nc.sbuf_tensor("S", [P, S_N], F32) as S:
            pass
        S_r = sb("S_r", [P, S_N], F32R)
        R1 = S[:, 0:14200]
        slot_at = lambda i: 14200 + NT * D + i * NC * D
        square = lambda v, at, n: v[:, at:at + n * D].rearrange("p (t d) -> p t d", d=D)
        xn = square(S, 14200, NT)
        slot = [square(S, slot_at(i), NC) for i in range(4)]
        PS = ctx.enter_context(nc.psum_tensor("PS", [P, 8, 512], F32))

        class Arena:

            def __init__(self, region, at=0):
                self.region, self.at = region, at

            def view(self, *dims):
                n = int(np.prod(dims))
                v = self.region[:, self.at:self.at + n]
                self.at += n
                if len(dims) == 1:
                    return v
                names = "abcd"[:len(dims)]
                return v.rearrange(f"p ({' '.join(names)}) -> p {' '.join(names)}",
                                   **{k: d for k, d in zip(names, dims)})

        m = Arena(R1)
        kT = m.view(NC, T)
        v64 = m.view(NT, D)
        s64 = [m.view(NP, 2, S1) for _ in range(2)]
        pT64 = m.view(NP, P)
        ctx0 = m.view(NC, T)
        flat = lambda v: v.rearrange("p a b -> p (a b)")
        m = Arena(R0)
        wgu = [m.view(NC, 2, I) for _ in range(2)]
        wgu.append(Arena(qbd[:, :, :, :].rearrange("p a b c -> p (a b c)")).view(NC, 2, I))
        wgu.append(Arena(R1, SX_AT).view(NC, 2, I))
        wdn = [m.view(3, D) for _ in range(3)]
        idle = Arena(flat(xnT[:, :, :]))
        wdn.append(idle.view(3, D))
        xgT = [m.view(NC, P), idle.view(NC, P)]
        xg = [xn[:, k, :] for k in range(NBUF)]
        yrow = [x[:, k, :] for k in range(NBUF)]
        act_g = m.view(I)
        hid = m.view(I)
        hT = m.view(3, P)
        sgate = [m.view(I) for _ in range(2)]
        shid = [m.view(I) for _ in range(2)]
        shT = hT
        assert m.at <= 13400, m.at
        m = Arena(R1)
        iota128 = m.view(P)
        upper = m.view(P)
        ones = m.view(P)
        zero512 = m.view(D)
        scores = m.view(NT, E)
        choice = m.view(NT, E)
        tmp64 = m.view(NT, E)
        srt = m.view(NT, NG, 8)
        gsum = m.view(NT, NG)
        gtop = m.view(NT, 8)
        gidx = m.view(NT, 8).bitcast(U32)
        gidxf = m.view(NT, 8)
        eqg = m.view(NT, NG, TG)
        gmask = m.view(NT * NG)
        top8 = m.view(NT, 8)
        idx8 = m.view(NT, 8).bitcast(U32)
        idx8f = m.view(NT * 8)
        eq = m.view(NT, 8, E)
        eqt = m.view(NT, 8, E)
        sel = m.view(NT, E)
        slotm = m.view(NT, E)
        wsum = m.view(NT)
        wnorm = m.view(NT)
        wk = m.view(NT * 8)
        slk = m.view(NT * 8)
        sdiv = m.view(NT * 8)
        smod = m.view(NT * 8)
        tokv = m.view(NT * 8)
        cnt = m.view(E)
        ntile = m.view(E)
        cum = m.view(E)
        base = m.view(E)
        cmp64 = m.view(E)
        oneA = [m.view(8, P) for _ in range(2)]
        eqB = m.view(8, NCOL)
        twoB = [m.view(8, 2, NCOL) for _ in range(2)]
        assert m.at <= 14200, m.at
        iotap = sb("iotap", [P, 1])
        pad_row = sb("pad_row", [P, 1])
        tok_id = sb("tok_id", [P, NT])
        idx_tab = sb("idx_tab", [P, NCOL], I32)
        w_tab = sb("w_tab", [P, NCOL])
        gcol = sb("gcol", [P, NBUF], I32)
        scol = sb("scol", [P, NBUF], I32)
        eot = sb("eot", [P, 2])
        eot_row = sb("eot_row", [1, P], I32)
        n_iter = sb("n_iter", [1, 1], I32)
        m = Arena(R0)
        kTx = [m.view(2, S2) for _ in range(2)]
        vx = [m.view(KT_N, D // 2) for _ in range(2)]
        assert m.at <= 13400, m.at
        m = Arena(R1)
        ctx_w = [w + -w % P for _, w in KC]
        ctx_raw = [m.view(NC, w) for w in ctx_w]
        top = Arena(S_r, m.at)
        ctx_hi = [top.view(NC, w) for w in ctx_w[:2]]
        ctx_hi += [square(S_r, 14200, NC), sb("ctx_hi3", [P, NC, ctx_w[3]], F32R)]
        m.at, low = top.at, Arena(S_r)
        ctx_lo = [low.view(NC, w) for w in ctx_w]
        assert m.at <= SX_AT
        m.at = SX_AT
        sx = [m.view(S2) for _ in range(2)]
        assert m.at <= 14200, m.at
        wkv_hi, wkv_lo = ([square(S_r, slot_at(i), NC) for i in ii] for ii in ((0, 2), (1, 3)))
        m = Arena(R0, 4 * S2 + KT_N * D // 2)
        wq1 = m.view(NC, D)
        pTx = [sb(f"pTx{i}", [P, 4, P]) for i in range(2)]
        qbh = [sb(f"qbh{i}", [P, 2, P]) for i in range(2)]
        mx4 = sb("mx4", [P, 4])
        nmx = sb("nmx", [P, 2])
        rsx = sb("rsx", [P, 2])
        rix = sb("rix", [P, 2])
        m = Arena(R0)
        rhs = m.view(NC, D)
        rabs = m.view(D)
        rscale = m.view(D)
        lscale = m.view(NT)
        linv = m.view(NT)
        rtmp = m.view(NC, D)
        rq = m.view(NC, D // 2).bitcast(BF16)
        lq = m.view(NC, T // 2).bitcast(BF16)

        ld_x = sem("ld_x"); ld_l0kv = sem("ld_l0kv"); ld_l0v = sem("ld_l0v"); ld_l0q = sem("ld_l0q"); ld_l0o = sem("ld_l0o")
        ld_bias = sem("ld_bias"); ld_small = sem("ld_small"); ld_p = sem("ld_p"); ld_boa = sem("ld_boa")
        ld_gate = sem("ld_gate"); ld_sh = sem("ld_sh"); ld_l1q = sem("ld_l1q"); ld_l1o = sem("ld_l1o")
        ld_l1a = sem("ld_l1a"); ld_l1ao = sem("ld_l1ao"); ld_bo1 = sem("ld_bo1"); ld_boa1 = sem("ld_boa1")
        ld_rhs = sem("ld_rhs"); ld_wkv = sem("ld_wkv"); ld_vb1 = sem("ld_vb1")
        consts = sem("consts"); pool_seq = sem("pool_seq"); dve_seq = sem("dve_seq")
        mv_ready = sem("mv_ready"); rstd_ready = sem("rstd_ready"); xn_ready = sem("xn_ready"); xt_made = sem("xt_made"); xT_ready = sem("xT_ready")
        xb_ready = sem("xb_ready"); q_made = sem("q_made"); q_ready = sem("q_ready")
        k_made = sem("k_made"); k_ready = sem("k_ready"); v_made = sem("v_made"); v_ready = sem("v_ready")
        sc_made = sem("sc_made"); sm_ready = sem("sm_ready"); p_ready = sem("p_ready")
        pt_made = sem("pt_made"); pt_act = sem("pt_act"); pt_dve = sem("pt_dve"); pv_made = sem("pv_made")
        z_ready = sem("z_ready"); zt_made = sem("zt_made"); zt_ready = sem("zt_ready")
        pj_made = sem("pj_made"); x_ready = sem("x_ready")
        wbd_ready = sem("wbd_ready"); zpad_set = sem("zpad_set"); rix_ready = sem("rix_ready"); dve_x = sem("dve_x")
        dve_seq3 = sem("dve_seq3"); dve_seq4 = sem("dve_seq4"); pool_seq4 = sem("pool_seq4")
        ff_x = sem("ff_x"); ff_y = sem("ff_y")
        lg_made = sem("lg_made"); lg_exp = sem("lg_exp"); sel_ready = sem("sel_ready"); rank_made = sem("rank_made")
        ab_ready = sem("ab_ready"); tab_made = sem("tab_made"); eot_ready = sem("eot_ready")
        eot_made = sem("eot_made"); tables = sem("tables"); rows_out = sem("rows_out"); acc_out = sem("acc_out")
        sh_g = sem("sh_g"); sh_u = sem("sh_u"); sh_silu = sem("sh_silu"); sh_h = sem("sh_h")
        sh_t = sem("sh_t"); sh_ht = sem("sh_ht"); sh_d = sem("sh_d"); sh_y = sem("sh_y")
        w_gu = [sem(f"w_gu{k}") for k in range(NBUF)]; w_dn = [sem(f"w_dn{k}") for k in range(NBUF)]; g_made = sem("g_made"); u_made = sem("u_made")
        silu_ready = sem("silu_ready"); h_ready = sem("h_ready"); ht_made = sem("ht_made")
        ht_ready = sem("ht_ready"); xg_loaded = [sem(f"xg_loaded{k}") for k in range(NBUF)]; xg_made = sem("xg_made")
        xg_ready = sem("xg_ready"); y_made = sem("y_made"); y_ready = sem("y_ready"); y_added = sem("y_added")
        gcol_set = sem("gcol_set"); scol_set = sem("scol_set"); acc_in = sem("acc_in")
        ctx_ld = [sem(f"ctx_ld{c}") for c in range(4)]
        mask_ld = sem("mask_ld"); mask_set = sem("mask_set")
        w_hi = sem("w_hi"); w_lo = sem("w_lo"); hi_ready = sem("hi_ready"); lo_ready = sem("lo_ready")
        pads_set = sem("pads_set"); kx_made = sem("kx_made"); kx_ready = sem("kx_ready"); vx_made = sem("vx_made"); vx_ready = sem("vx_ready")
        qh_ready = sem("qh_ready"); sx_made = sem("sx_made"); sx_read = sem("sx_read"); sx_max = sem("sx_max")
        px_ready = sem("px_ready"); ptx_made = sem("ptx_made"); ptx_act = sem("ptx_act"); ptx_dve = sem("ptx_dve")
        pvx_part = sem("pvx_part"); zx_ready = sem("zx_ready")
        ztx_made = sem("ztx_made"); ztx_ready = sem("ztx_ready"); xx_ready = sem("xx_ready")
        rq_ready = sem("rq_ready"); lq_made = sem("lq_made"); lq_ready = sem("lq_ready")
        ff_made = sem("ff_made"); rabs_ready = sem("rabs_ready"); rmax_ready = sem("rmax_ready"); out_done = sem("out_done")
        pj1_made = sem("pj1_made")

        class Chain:

            def __init__(self, eng, s):
                self.eng, self.s, self.n = eng, s, 0

            def __call__(self, ins):
                ins.then_inc(self.s, 1)
                self.n += 1
                self.eng.wait_ge(self.s, self.n)

        def count(eng, value):
            return value if isinstance(value, int) else eng.snap(eng.to_reg(value))


        def ln_dve(dve, link, n):
            for t in range(NT):
                last = nc.vector.bn_stats(st[:, t, :], x[:, t, :])
            link(last)
            for t in range(NT):
                last = nc.vector.bn_aggr(mv[:, t, :], st[:, t, :])
            link(last)
            nc.vector.tensor_scalar(rstd[:, :], mv[:, :, 1], EPS, None, ALU.add).then_inc(mv_ready, 1)
            dve.wait_ge(rstd_ready, n + 1)
            for t in range(NT):
                nc.vector.tensor_scalar(xn[:, t, :], x[:, t, :], mv[:, t, 0:1], rstd[:, t:t + 1],
                                        ALU.subtract, ALU.mult).then_inc(xn_ready, 1)

        def ln_pool(pool, n):
            pool.wait_ge(mv_ready, n + 1)
            nc.gpsimd.tensor_tensor(rstd[:, :], rstd[:, :], neg_half[:, :], ALU.pow).then_inc(rstd_ready, 1)

        def xt_pe(pe, n):
            for t in range(NT):
                pe.wait_ge(xn_ready, NT * n + t + 1)
                for c in range(NC):
                    last = nc.tensor.transpose(PS[:, t, c * P:(c + 1) * P], xn[:, t, c * P:(c + 1) * P], ident[:, :])
                last.then_inc(xt_made, 1)

        def xt_copy(eng, copy, n, tiles):
            for t in tiles:
                eng.wait_ge(xt_made, NT * n + t + 1)
                copy(xnT[:, :, t * P:(t + 1) * P],
                     PS[:, t, :].rearrange("p (c k) -> p c k", c=NC)).then_inc(xT_ready, 1)

        def q_pe(pe, w, n, L):
            pe.wait_ge(xT_ready, NT * (n + 1))
            for dc in range(NC):
                for c in range(NC):
                    last = nc.tensor.matmul(PS[:, 4 + dc, :], w[:, c, dc * P:(dc + 1) * P], xnT[:, c, :],
                                            start=(c == 0), stop=(c == NC - 1))
                last.then_inc(q_made, 1)

        def q_dve(dve, L, bias):
            for dc in range(NC):
                dve.wait_ge(q_made, NC * L + dc + 1)
                src = PS[:, 4 + dc, :].rearrange("p (b q) -> p b q", b=B)
                for h in range(2):
                    dst = qbd[:, dc, :, h * S1:(h + 1) * S1]
                    if bias is None:
                        last = nc.vector.tensor_scalar(dst, src, halfmask[:, h:h + 1], None, ALU.mult)
                    else:
                        last = nc.vector.tensor_scalar(dst, src, bias_c[:, bias, dc:dc + 1], halfmask[:, h:h + 1],
                                                       ALU.add, ALU.mult)
                last.then_inc(q_ready, 1)

        def att_pe(pe, L, wo):
            def sc(t):
                b0 = 2 * (t % 2)
                if t >= 2:
                    pe.wait_ge(sm_ready, L * NT + t - 1)
                for par in range(2):
                    b = 2 * t + par
                    for m in range(NP):
                        r, dc = 64 * (m // 4), m % 4
                        c0 = (2 * dc + par) * S1
                        last = nc.tensor.matmul(PS[:, b0 + m // 4, c0:c0 + S1],
                                                qbd[r:r + 64, dc, b, :], kT[r:r + 64, dc, b * S1:(b + 1) * S1],
                                                start=True, stop=True)
                last.then_inc(sc_made, 1)

            sc(0)
            sc(1)
            for t in range(NT):
                k = L * NT + t + 1
                pe.wait_ge(p_ready, k)
                for pr in range(NP):
                    if pr == 4 and t:
                        pe.wait_ge(x_ready, k - 1)
                    last = nc.tensor.transpose(PS[:, 4 + pr // 4, (pr % 4) * P:(pr % 4 + 1) * P],
                                               s64[t % 2][:, pr, :, :].rearrange("p a b -> p (a b)"), ident[:, :])
                    if pr % 4 == 3:
                        last.then_inc(pt_made, 1)
                pe.wait_ge(pt_act, k)
                pe.wait_ge(pt_dve, k)
                for par in range(2):
                    for m in range(NP):
                        v0 = (2 * (m % 4) + m // 4) * 64
                        last = nc.tensor.matmul(PS[:, 6 + par, m * 64:(m + 1) * 64],
                                                pT64[64 * par:64 * par + 64, m, :],
                                                v64[64 * par:64 * par + 64, t, v0:v0 + 64],
                                                start=True, stop=True)
                last.then_inc(pv_made, 1)
                if t + 2 < NT:
                    sc(t + 2)
                pe.wait_ge(z_ready, k)
                for par in range(2):
                    for jj in range(2):
                        last = nc.tensor.transpose(PS[:, 4, (2 * par + jj) * P:(2 * par + jj + 1) * P],
                                                   z[:, par, 4 * jj:4 * jj + 4, :].rearrange("p a b -> p (a b)"),
                                                   ident[:, :])
                last.then_inc(zt_made, 1)
                pe.wait_ge(zt_ready, k)
                for jh in range(4):
                    last = nc.tensor.matmul(PS[:, 5, :], zT[:, jh // 2, jh % 2, t * P:(t + 1) * P], wo[:, jh, :],
                                            start=(jh == 0), stop=(jh == 3))
                last.then_inc(pj_made, 1)
            pe.wait_ge(x_ready, (L + 1) * NT)

        def att_act(act, L, scale):
            def ex(t):
                act.wait_ge(sm_ready, L * NT + t + 1)
                sv = s64[t % 2].rearrange("p a b c -> p (a b c)")
                nc.scalar.activation(sv, sv, ACT.Exp, scale=scale).then_inc(p_ready, 1)

            ex(0)
            ex(1)
            for t in range(NT):
                k = L * NT + t + 1
                act.wait_ge(pt_made, 2 * (k - 1) + 1)
                nc.scalar.copy(pT64[:, 0:4, :].rearrange("p a b -> p (a b)"), PS[:, 4, :]).then_inc(pt_act, 1)
                act.wait_ge(zt_made, k)
                for par in range(2):
                    b = 2 * t + par
                    last = nc.scalar.copy(
                        zT[:, :, :, b * S1:(b + 1) * S1],
                        PS[:, 4, par * 256:(par + 1) * 256].rearrange("p (j h q) -> p j h q", j=2, h=2))
                last.then_inc(zt_ready, 1)
                if t + 2 < NT:
                    ex(t + 2)

        def att_dve(dve, link, L, masked, between=()):
            def pre(t):
                dve.wait_ge(sc_made, L * NT + t + 1)
                src = PS[:, 2 * (t % 2):2 * (t % 2) + 2, :].rearrange("p a (r b k) -> p (a r) b k", b=2, k=S1)
                s, mx = s64[t % 2], smx[:, t % 2, :].rearrange("p (a b) -> p a b", a=NP)
                if masked:
                    link(nc.vector.tensor_tensor(s, src, causal[:, :].unsqueeze(1).unsqueeze(1)
                                                 .to_broadcast([P, NP, 2, S1]), ALU.add))
                    src = s
                link(nc.vector.tensor_reduce(mx, src, AX.X, ALU.max))
                nc.vector.tensor_tensor(s, src, mx.unsqueeze(3).to_broadcast([P, NP, 2, S1]),
                                        ALU.subtract).then_inc(sm_ready, 1)

            pre(0)
            pre(1)
            for t in range(NT):
                k = L * NT + t + 1
                dve.wait_ge(pt_made, 2 * k)
                nc.vector.tensor_copy(pT64[:, 4:8, :].rearrange("p a b -> p (a b)"), PS[:, 5, :]).then_inc(pt_dve, 1)
                dve.wait_ge(p_ready, k)
                link(nc.vector.tensor_reduce(ssum[:, :].rearrange("p (a b) -> p a b", a=NP), s64[t % 2],
                                             AX.X, ALU.add))
                link(nc.vector.reciprocal(rinv[:, :], ssum[:, :]))
                dve.wait_ge(pv_made, k)
                for h in range(2):
                    r = slice(64 * h, 64 * h + 64)
                    last = nc.vector.tensor_tensor(
                        z[r, :, :, :],
                        PS[r, 6:8, :].rearrange("p a (r h d) -> p a r h d", h=2, d=HD)[:, :, :, h, :],
                        rinv[r, :].rearrange("p (r a) -> p a r", a=2).unsqueeze(3).to_broadcast([64, 2, NP, HD]),
                        ALU.mult)
                last.then_inc(z_ready, 1)
                if t + 2 < NT:
                    pre(t + 2)
                if t < len(between):
                    between[t]()
                dve.wait_ge(pj_made, k)
                dve.wait_ge(xb_ready, XB[L])
                nc.vector.tensor_tensor(x[:, t, :], x[:, t, :], PS[:, 5, :], ALU.add).then_inc(x_ready, 1)
            dve.wait_ge(x_ready, (L + 1) * NT)

        XB = [1, 2, 4]

        def add_out_bias(pool, n, after):
            pool.wait_ge(xn_ready, NT * after)
            nc.gpsimd.tensor_tensor(x[:, :, :], x[:, :, :],
                                    bias_r[:, :].unsqueeze(1).to_broadcast([P, NT, D]), ALU.add).then_inc(xb_ready, 1)

        with nc.Block() as block:
            @block.sync
            def _(sp):
                sp.dma_start(ctx0, a["ctx0"]).then_inc(ld_l0kv, 16)
                sp.dma_start(slot[1][:, :, :], a["l0_wk"]).then_inc(ld_l0kv, 16)
                sp.dma_start(bias_c[:, :, :], a["bias_c"]).then_inc(ld_bias, 16)
                sp.dma_start(x[:, :, :], a["x"]).then_inc(ld_x, 16)
                sp.dma_start(slot[2][:, :, :], a["l0_wv"]).then_inc(ld_l0v, 16)
                sp.dma_start(vbias[:, :], a["l0_bv"].to_broadcast([P, D])).then_inc(ld_bias, 16)
                sp.dma_start(slot[0][:, :, :], a["l0_wq"]).then_inc(ld_l0q, 16)
                sp.dma_start(bias_r[:, :], a["l0_bo"].to_broadcast([P, D])).then_inc(ld_bias, 16)
                sp.dma_start(slot[3][:, :, :], a["l0_wo"]).then_inc(ld_l0o, 16)
                sp.dma_start(wsmall[:, :, :], a["l0a_wq"]).then_inc(ld_small, 16)
                sp.dma_start(gatew[:, :, :], a["gate_w"]).then_inc(ld_gate, 16)
                sp.dma_start(gbias[:, :], a["gate_b"].to_broadcast([P, E])).then_inc(ld_gate, 16)
                for k in range(2):
                    sp.dma_start(wgu[k], a["w_gu"][E + k]).then_inc(ld_sh, 16)
                    sp.dma_start(wdn[k][:, 0:2, :], a["w_dna"][E + k]).then_inc(ld_sh, 16)
                    sp.dma_start(wdn[k][0:96, 2, :], a["w_dnb"][E + k]).then_inc(ld_sh, 16)
                sp.wait_ge(k_made, NC)
                sp.dma_start(slot[1][:, :, :], a["l0a_wp"]).then_inc(ld_p, 16)
                sp.wait_ge(xb_ready, 1)
                sp.dma_start(bias_r[:, :], a["l0a_bp"].to_broadcast([P, D])).then_inc(ld_boa, 16)
                sp.wait_ge(v_ready, NT)
                sp.dma_start(vbias[:, :], a["l1_bv"].to_broadcast([P, D])).then_inc(ld_vb1, 16)
                sp.dma_start(mask8[:, :], a["mask"][0:1, :].to_broadcast([P, S2])).then_inc(mask_ld, 16)
                for i in range(2):
                    sp.wait_ge(pj_made, NT * (2 - i))
                    sp.dma_start(slot[1 + 2 * i][:, :, :], a["l1_wkv"][:, :, i * D:(i + 1) * D]).then_inc(ld_wkv, 16)
                sp.wait_ge(consts, 1)
                sp.wait_ge(xn_ready, 3 * NT)
                sp.wait_ge(zpad_set, 1)
                sp.dma_start(xrow[0:T, :].rearrange("(t p) d -> p t d", p=P), xn[:, :, :]).then_inc(rows_out, 16)
                sp.dma_start(xrow[T:T + P, :], zero512).then_inc(rows_out, 16)
                sp.dma_start(acc[T:T + P, :], zero512).then_inc(acc_out, 16)
                sp.wait_ge(rows_out, 32)
                sp.wait_ge(acc_out, 16)

            @block.gpsimd
            def _(pool):
                link = Chain(pool, pool_seq)
                link(nc.gpsimd.memset(neg_half[:, :], -0.5))
                link(nc.gpsimd.memset(ident[:, :], 0.0))
                link(nc.gpsimd.affine_select(out=ident[:, :], in_=ident[:, :], compare_op=ALU.not_equal, fill=1.0,
                                             base=0, pattern=[[-1, P]], channel_multiplier=1))
                link(nc.gpsimd.memset(causal[:, :], 0.0))
                for h in range(2):
                    r = slice(64 * h, 64 * h + 64)
                    link(nc.gpsimd.affine_select(out=causal[r, :], in_=causal[r, :], compare_op=ALU.is_ge, fill=NEG,
                                                 base=0, pattern=[[-1, S1]], channel_multiplier=1))
                for g in range(4):
                    r = slice(32 * g, 32 * g + 32)
                    link(nc.gpsimd.memset(halfmask[r, 0:1], 1.0 - g % 2))
                    link(nc.gpsimd.memset(halfmask[r, 1:2], float(g % 2)))
                link(nc.gpsimd.memset(wbd[:, :, :], 0.0))
                link(nc.gpsimd.iota(iotap[:, :], [[0, 1]], base=0, channel_multiplier=1,
                                    allow_small_or_imprecise_dtypes=True))
                link(nc.gpsimd.iota(pad_row[:, :], [[0, 1]], base=T, channel_multiplier=1,
                                    allow_small_or_imprecise_dtypes=True))
                link(nc.gpsimd.iota(tok_id[:, :], [[P, NT]], base=-T, channel_multiplier=1,
                                    allow_small_or_imprecise_dtypes=True))
                nc.gpsimd.memset(eot[:, :], 0.0).then_inc(consts, 1)
                ln_pool(pool, 0)
                pool.wait_ge(ld_small, 16)
                for g in range(4):
                    r = slice(32 * g, 32 * g + 32)
                    nc.gpsimd.tensor_copy(wbd[r, :, 32 * g:32 * g + 32], wsmall[r, :, :]).then_inc(wbd_ready, 1)
                    pool.wait_ge(wbd_ready, g + 1)
                pool.wait_ge(ld_bias, 48)
                add_out_bias(pool, 0, 1)
                ln_pool(pool, 1)
                pool.wait_ge(ld_boa, 16)
                add_out_bias(pool, 1, 2)
                ln_pool(pool, 2)
                pool.wait_ge(pj_made, 2 * NT)
                link(nc.gpsimd.iota(iota128, [[1, P]], base=0, channel_multiplier=0,
                                    allow_small_or_imprecise_dtypes=True))
                link(nc.gpsimd.memset(ones, 1.0))
                link(nc.gpsimd.memset(upper, 1.0))
                link(nc.gpsimd.affine_select(out=upper, in_=upper, compare_op=ALU.is_gt, fill=0.0,
                                             base=0, pattern=[[1, P]], channel_multiplier=-1))
                nc.gpsimd.memset(zero512, 0.0).then_inc(zpad_set, 1)

            @block.tensor
            def _(pe):
                pe.wait_ge(ld_l0kv, 32)
                for dc in range(NC):
                    for c in range(NC):
                        last = nc.tensor.matmul(PS[:, dc, :], slot[1][:, c, dc * P:(dc + 1) * P], ctx0[:, c, :],
                                                start=(c == 0), stop=(c == NC - 1))
                    last.then_inc(k_made, 1)
                pe.wait_ge(ld_l0v, 16)
                for t in range(NT):
                    for c in range(NC):
                        last = nc.tensor.matmul(PS[:, 4 + t, :], ctx0[:, c, t * P:(t + 1) * P], slot[2][:, c, :],
                                                start=(c == 0), stop=(c == NC - 1))
                    last.then_inc(v_made, 1)
                pe.wait_ge(consts, 1)
                pe.wait_ge(k_ready, NC)
                xt_pe(pe, 0)
                pe.wait_ge(v_ready, NT)
                pe.wait_ge(ld_l0q, 16)
                q_pe(pe, slot[0], 0, 0)
                pe.wait_ge(q_ready, NC)
                pe.wait_ge(ld_l0o, 16)
                att_pe(pe, 0, slot[3])

                xt_pe(pe, 1)
                pe.wait_ge(xT_ready, 2 * NT)
                pe.wait_ge(wbd_ready, 4)
                for dc in range(NC):
                    nc.tensor.matmul(PS[:, 4 + dc, :], wbd[:, dc, :], xnT[:, dc, :],
                                     start=True, stop=True).then_inc(q_made, 1)
                for t in range(NT):
                    for dc in range(NC):
                        last = nc.tensor.matmul(PS[:, t, dc * P:(dc + 1) * P], xnT[:, dc, t * P:(t + 1) * P],
                                                wbd[:, dc, :], start=True, stop=True)
                    last.then_inc(v_made, 1)
                pe.wait_ge(q_ready, 2 * NC)
                pe.wait_ge(v_ready, 2 * NT)
                pe.wait_ge(ld_p, 16)
                att_pe(pe, 1, slot[1])

                xt_pe(pe, 2)
                pe.wait_ge(xT_ready, 3 * NT)
                pe.wait_ge(ld_gate, 32)
                for t in range(NT):
                    for c in range(NC):
                        last = nc.tensor.matmul(PS[:, 0, t * E:(t + 1) * E], xnT[:, c, t * P:(t + 1) * P],
                                                gatew[:, c, :], start=(c == 0), stop=(c == NC - 1))
                last.then_inc(lg_made, 1)

                def shared_in(k):
                    t, hf = k // 2, k % 2
                    if k >= 2:
                        pe.wait_ge(sh_silu, k - 1)
                        pe.wait_ge(sh_h, k - 1)
                    for gu in range(2):
                        for c in range(NC):
                            last = nc.tensor.matmul(PS[:, 2 + 2 * hf + gu, 0:I], xnT[:, c, t * P:(t + 1) * P],
                                                    wgu[hf][:, c, gu, :], start=(c == 0), stop=(c == NC - 1))
                        last.then_inc(sh_u if gu else sh_g, 1)

                def shared_out(k):
                    t, hf = k // 2, k % 2
                    pe.wait_ge(sh_h, k + 1)
                    if k >= 1:
                        pe.wait_ge(sh_ht, k)
                    for j, (i0, n) in enumerate(IJ):
                        last = nc.tensor.transpose(PS[0:n, 6, j * P:(j + 1) * P], shid[hf][:, i0:i0 + n], ident[:, :])
                    last.then_inc(sh_t, 1)
                    pe.wait_ge(sh_ht, k + 1)
                    if hf == 0 and t >= 1:
                        pe.wait_ge(sh_y, t)
                    for j, (i0, n) in enumerate(IJ):
                        last = nc.tensor.matmul(PS[:, 7, :], shT[0:n, j, :], wdn[hf][0:n, j, :],
                                                start=(hf == 0 and j == 0), stop=(hf == 1 and j == 2))
                    last.then_inc(sh_d, 1)

                pe.wait_ge(ld_sh, 96)
                shared_in(0)
                shared_in(1)
                shared_out(0)
                shared_in(2)
                shared_out(1)
                shared_in(3)
                shared_out(2)
                pe.wait_ge(sel_ready, 1)
                for t in range(NT):
                    for u in range(t + 1):
                        nc.tensor.matmul(PS[:, 0, t * E:(t + 1) * E], ones if u < t else upper, sel[:, u, :],
                                         start=(u == 0), stop=(u == t))
                for u in range(NT):
                    last = nc.tensor.matmul(PS[:, 0, NT * E:(NT + 1) * E], ones, sel[:, u, :],
                                            start=(u == 0), stop=(u == NT - 1))
                last.then_inc(rank_made, 1)
                shared_in(4)
                shared_out(3)
                shared_in(5)
                shared_out(4)
                pe.wait_ge(eot_ready, 1)
                nc.tensor.transpose(PS[0:2, 0, 0:P], eot[:, :], ident[:, :]).then_inc(eot_made, 1)
                shared_in(6)
                shared_out(5)
                shared_in(7)
                shared_out(6)
                for t in range(NT):
                    pe.wait_ge(ab_ready, t + 1)
                    for k in range(8):
                        last = nc.tensor.matmul(PS[:, 1, 0:2 * NCOL], oneA[t % 2][:, k, :],
                                                twoB[t % 2][:, k, :, :].rearrange("p a b -> p (a b)"),
                                                start=(t == 0 and k == 0), stop=(t == NT - 1 and k == 7))
                    last.then_inc(tab_made, 1)
                shared_out(7)

            def shared_ht(act, k):
                act.wait_ge(sh_t, k + 1)
                if k >= 1:
                    act.wait_ge(sh_d, k)
                nc.scalar.copy(shT[:, 0:2, :], PS[:, 6, 0:2 * P].rearrange("p (a b) -> p a b", a=2))
                nc.scalar.copy(shT[0:96, 2, :], PS[0:96, 6, 2 * P:3 * P]).then_inc(sh_ht, 1)

            @block.scalar
            def _(act):
                act.wait_ge(ld_bias, 48)
                for dc in range(NC):
                    act.wait_ge(k_made, dc + 1)
                    nc.scalar.activation(kT[:, dc, :], PS[:, dc, :], ACT.Identity,
                                         bias=bias_c[:, 1, dc:dc + 1]).then_inc(k_ready, 1)
                xt_copy(act, nc.scalar.copy, 0, (0, 2))
                att_act(act, 0, SC)
                xt_copy(act, nc.scalar.copy, 1, (0, 2))
                for dc in range(NC):
                    act.wait_ge(q_made, NC + dc + 1)
                    nc.scalar.copy(kT[:, dc, :], PS[:, 4 + dc, :]).then_inc(k_ready, 1)
                for t in range(NT):
                    act.wait_ge(v_made, NT + t + 1)
                    nc.scalar.copy(v64[:, t, :], PS[:, t, :]).then_inc(v_ready, 1)
                att_act(act, 1, 1.0 / SC)
                xt_copy(act, nc.scalar.copy, 2, (0, 2))
                act.wait_ge(lg_made, 1)
                nc.scalar.activation(scores.rearrange("p a b -> p (a b)"), PS[:, 0, 0:NT * E], ACT.Exp,
                                     scale=-1.0).then_inc(lg_exp, 1)
                for k in range(2 * NT):
                    hf = k % 2
                    act.wait_ge(sh_g, k + 1)
                    if k >= 2:
                        act.wait_ge(sh_h, k - 1)
                    nc.scalar.activation(sgate[hf], PS[:, 2 + 2 * hf, 0:I], ACT.Silu).then_inc(sh_silu, 1)
                    if k >= 1:
                        shared_ht(act, k - 1)
                shared_ht(act, 2 * NT - 1)

            @block.vector
            def _(dve):
                link = Chain(dve, dve_seq)
                dve.wait_ge(ld_x, 16)
                ln_dve(dve, link, 0)
                dve.wait_ge(ld_bias, 48)
                for t in range(NT):
                    dve.wait_ge(v_made, t + 1)
                    nc.vector.tensor_tensor(v64[:, t, :], PS[:, 4 + t, :], vbias[:, :], ALU.add).then_inc(v_ready, 1)
                xt_copy(dve, nc.vector.tensor_copy, 0, (1, 3))
                dve.wait_ge(consts, 1)
                q_dve(dve, 0, 0)
                att_dve(dve, link, 0, True)

                ln_dve(dve, link, 1)
                xt_copy(dve, nc.vector.tensor_copy, 1, (1, 3))
                for dc in range(NC):
                    dve.wait_ge(k_ready, NC + dc + 1)
                    for h in range(2):
                        last = nc.vector.tensor_scalar(qbd[:, dc, :, h * S1:(h + 1) * S1],
                                                       kT[:, dc, :].rearrange("p (b q) -> p b q", b=B),
                                                       halfmask[:, h:h + 1], None, ALU.mult)
                    last.then_inc(q_ready, 1)
                att_dve(dve, link, 1, False)

                ln_dve(dve, link, 2)
                xt_copy(dve, nc.vector.tensor_copy, 2, (1, 3))

                def shared_mul(k):
                    hf = k % 2
                    dve.wait_ge(sh_silu, k + 1)
                    dve.wait_ge(sh_u, k + 1)
                    if k >= 2:
                        dve.wait_ge(sh_t, k - 1)
                    nc.vector.tensor_tensor(shid[hf], sgate[hf], PS[:, 3 + 2 * hf, 0:I], ALU.mult).then_inc(sh_h, 1)

                def shared_add(t):
                    dve.wait_ge(sh_d, 2 * t + 2)
                    nc.vector.tensor_tensor(x[:, t, :], x[:, t, :], PS[:, 7, :], ALU.add).then_inc(sh_y, 1)

                fl = lambda v: v.rearrange("p a b -> p (a b)")
                dve.wait_ge(lg_exp, 1)
                dve.wait_ge(ld_gate, 32)
                dve.wait_ge(zpad_set, 1)
                link(nc.vector.tensor_scalar(fl(scores), fl(scores), 1.0, None, ALU.add))
                link(nc.vector.reciprocal(fl(scores), fl(scores)))
                link(nc.vector.tensor_tensor(choice, scores, gbias[:, :].unsqueeze(1).to_broadcast([P, NT, E]), ALU.add))
                for t in range(NT):
                    for g in range(NG):
                        last = nc.vector.max(srt[:, t, g, :], choice[:, t, 8 * g:8 * g + 8])
                link(last)
                link(nc.vector.tensor_tensor(gsum, srt[:, :, :, 0], srt[:, :, :, 1], ALU.add))
                for t in range(NT):
                    last = nc.vector.max(gtop[:, t, :], gsum[:, t, :])
                link(last)
                for t in range(NT):
                    last = nc.vector.max_index(gidx[:, t, :], gtop[:, t, :], gsum[:, t, :])
                link(last)
                shared_mul(0)
                shared_mul(1)
                link(nc.vector.tensor_copy(gidxf, gidx))
                link(nc.vector.tensor_tensor(
                    eqg, iota128[:, 0:NG].unsqueeze(1).unsqueeze(3).to_broadcast([P, NT, NG, TG]),
                    gidxf[:, :, 0:TG].unsqueeze(2).to_broadcast([P, NT, NG, TG]), ALU.is_equal))
                link(nc.vector.tensor_reduce(gmask.rearrange("p (a b) -> p a b", a=NT), eqg, AX.X, ALU.max))
                link(nc.vector.tensor_tensor(
                    tmp64.rearrange("p a (g k) -> p (a g) k", g=NG), choice.rearrange("p a (g k) -> p (a g) k", g=NG),
                    gmask.unsqueeze(2).to_broadcast([P, NT * NG, 8]), ALU.mult))
                for t in range(NT):
                    last = nc.vector.max(top8[:, t, :], tmp64[:, t, :])
                link(last)
                for t in range(NT):
                    last = nc.vector.max_index(idx8[:, t, :], top8[:, t, :], tmp64[:, t, :])
                link(last)
                link(nc.vector.tensor_copy(idx8f.rearrange("p (a b) -> p a b", a=NT), idx8))
                eqf, eqtf = (v.rearrange("p a b e -> p (a b) e") for v in (eq, eqt))
                link(nc.vector.tensor_tensor(eqf, iota128[:, 0:E].unsqueeze(1).to_broadcast([P, NT * 8, E]),
                                             idx8f.unsqueeze(2).to_broadcast([P, NT * 8, E]), ALU.is_equal))
                nc.vector.tensor_reduce(sel, eq.rearrange("p a k e -> p a e k"), AX.X, ALU.add).then_inc(sel_ready, 1)
                dve.wait_ge(sel_ready, 1)
                shared_mul(2)
                shared_mul(3)
                shared_add(0)
                link(nc.vector.tensor_tensor(tmp64, sel, scores, ALU.mult))
                link(nc.vector.tensor_reduce(wsum, tmp64, AX.X, ALU.add))
                link(nc.vector.tensor_scalar(wsum, wsum, 1e-20, None, ALU.add))
                link(nc.vector.reciprocal(wnorm, wsum))
                link(nc.vector.tensor_scalar(wnorm, wnorm, ROUTED_SCALE, None, ALU.mult))
                link(nc.vector.tensor_tensor(tmp64, tmp64, wnorm.unsqueeze(2).to_broadcast([P, NT, E]), ALU.mult))
                link(nc.vector.tensor_tensor(eqt, eq, tmp64.unsqueeze(2).to_broadcast([P, NT, 8, E]), ALU.mult))
                link(nc.vector.tensor_reduce(wk, eqtf, AX.X, ALU.add))
                dve.wait_ge(rank_made, 1)
                link(nc.vector.tensor_copy(cnt, PS[:, 0, NT * E:(NT + 1) * E]))
                link(nc.vector.tensor_scalar(ntile, cnt, 0.0, None, ALU.is_gt))
                for j in range(1, T // P):
                    link(nc.vector.scalar_tensor_tensor(out=ntile, in0=cnt, scalar=float(j * P), in1=ntile,
                                                        op0=ALU.is_gt, op1=ALU.add))
                link(nc.vector.memset(base, 0.0))
                link(nc.vector.tensor_tensor_scan(cum, ntile, base, 0.0, ALU.add, ALU.add))
                link(nc.vector.tensor_tensor(base, cum, ntile, ALU.subtract))
                link(nc.vector.tensor_scalar(base, base, float(P), None, ALU.mult))
                link(nc.vector.tensor_tensor(slotm, PS[:, 0, 0:NT * E].rearrange("p (a b) -> p a b", a=NT),
                                             base.unsqueeze(1).to_broadcast([P, NT, E]), ALU.add))
                link(nc.vector.tensor_scalar(cmp64, cum, iotap[:, 0:1], None, ALU.is_le))
                link(nc.vector.tensor_reduce(eot[:, 0:1], cmp64, AX.X, ALU.add))
                nc.vector.tensor_scalar(eot[:, 0:1], eot[:, 0:1], float(E - 1), None, ALU.min).then_inc(eot_ready, 1)
                shared_mul(4)
                shared_mul(5)
                shared_add(1)
                link(nc.vector.tensor_tensor(eqt, eq, slotm.unsqueeze(2).to_broadcast([P, NT, 8, E]), ALU.mult))
                link(nc.vector.tensor_reduce(slk, eqtf, AX.X, ALU.add))
                link(nc.vector.tensor_scalar(sdiv, slk, 1.0 / P, -63.5 / P, ALU.mult, ALU.add))
                link(nc.vector.tensor_scalar(sdiv, sdiv, ROUND, None, ALU.add))
                link(nc.vector.tensor_scalar(sdiv, sdiv, -ROUND, None, ALU.add))
                link(nc.vector.scalar_tensor_tensor(out=smod, in0=sdiv, scalar=-float(P), in1=slk,
                                                    op0=ALU.mult, op1=ALU.add))
                link(nc.vector.tensor_tensor(tokv.rearrange("p (a b) -> p a b", a=NT),
                                             tok_id[:, :].unsqueeze(2).to_broadcast([P, NT, 8]),
                                             smod.rearrange("p (a b) -> p a b", a=NT), ALU.subtract))
                shared_mul(6)
                shared_add(2)
                shared_mul(7)
                for t in range(NT):
                    k8 = slice(8 * t, 8 * t + 8)
                    if t >= 2:
                        dve.wait_ge(tab_made, t - 1)
                    if t >= 1:
                        dve.wait_ge(ab_ready, t)
                    nc.vector.tensor_tensor(oneA[t % 2], iota128.unsqueeze(1).to_broadcast([P, 8, P]),
                                            smod[:, k8].unsqueeze(2).to_broadcast([P, 8, P]), ALU.is_equal)
                    link(nc.vector.tensor_tensor(eqB, iota128[:, 0:NCOL].unsqueeze(1).to_broadcast([P, 8, NCOL]),
                                                 sdiv[:, k8].unsqueeze(2).to_broadcast([P, 8, NCOL]), ALU.is_equal))
                    nc.vector.tensor_tensor(twoB[t % 2][:, :, 0, :], eqB,
                                            tokv[:, k8].unsqueeze(2).to_broadcast([P, 8, NCOL]), ALU.mult)
                    nc.vector.tensor_tensor(twoB[t % 2][:, :, 1, :], eqB,
                                            wk[:, k8].unsqueeze(2).to_broadcast([P, 8, NCOL]),
                                            ALU.mult).then_inc(ab_ready, 1)
                dve.wait_ge(eot_made, 1)
                nc.vector.tensor_copy(eot_row[:, :], PS[0:1, 0, 0:P])
                link(nc.vector.tensor_scalar(wsum[:, 0:1], cum[:, E - 1:E], 1.0 / NBUF, 0.5 - 0.5 / NBUF,
                                             ALU.mult, ALU.add))
                link(nc.vector.tensor_scalar(wsum[:, 0:1], wsum[:, 0:1], ROUND, None, ALU.add))
                link(nc.vector.tensor_scalar(wsum[:, 0:1], wsum[:, 0:1], -ROUND - 2.0, None, ALU.add))
                nc.vector.tensor_copy(n_iter[:, :], wsum[0:1, 0:1])
                dve.wait_ge(tab_made, NT)
                nc.vector.tensor_scalar(idx_tab[:, :], PS[:, 1, 0:NCOL], pad_row[:, 0:1], None, ALU.add)
                nc.vector.tensor_copy(w_tab[:, :], PS[:, 1, NCOL:2 * NCOL]).then_inc(tables, 1)
                shared_add(3)
                dve.wait_ge(tables, 1)
                dve.wait_ge(sh_y, NT)

        def iterations(eng):
            return eng.value_load(n_iter[0:1, 0:1], min_val=T * TOPK // P // NBUF - 2, max_val=NCOL // NBUF - 2) + 2

        def tile_before(r, k):
            return (r, k - 1) if k else (r - 1, NBUF - 1)

        def tile_after(r, k):
            return (r, k + 1) if k < NBUF - 1 else (r + 1, 0)

        def column(r, k):
            return slice(NBUF * r + k, NBUF * r + k + 1) if isinstance(r, int) else bass.ds(NBUF * r + k, 1)

        with nc.Block() as block:
            @block.sync
            def _(sp):
                def load(r, k):
                    i = NBUF * r + k
                    e = sp.value_load(eot_row[0:1, column(r, k)], min_val=0, max_val=E - 1)
                    ev = bass.ds(e, 1)
                    if not isinstance(r, int):
                        sp.wait_ge(u_made, i - NBUF + 1)
                    sp.dma_start(wgu[k].rearrange("p c g i -> p (c g i)"),
                                 a["w_gu2"][ev, :, :].rearrange("e p n -> (e p) n")).then_inc(w_gu[k], 16)
                    if not isinstance(r, int):
                        sp.wait_ge(y_made, i - NBUF + 1)
                    sp.dma_start(wdn[k][:, 0:2, :].rearrange("p c n -> p (c n)"),
                                 a["w_dna2"][ev, :, :].rearrange("e p n -> (e p) n")).then_inc(w_dn[k], 16)
                    sp.dma_start(wdn[k][0:96, 2, :],
                                 a["w_dnb"][ev, :, :].rearrange("e p n -> (e p) n")).then_inc(w_dn[k], 16)

                n = iterations(sp)
                for k in range(NBUF):
                    load(0, k)
                    if k == 0:
                        sp.dma_start(acc[0:T, :].rearrange("(t p) d -> p t d", p=P), x[:, :, :]).then_inc(acc_out, 16)
                with sp.Fori(1, n) as r:
                    for k in range(NBUF):
                        load(r, k)
                for c, (k0, w) in enumerate(KC):
                    sp.dma_start(ctx_raw[c][:, :, 0:w], a["ctxT"][0, :, :, k0:k0 + w]).then_inc(ctx_ld[c], 16)
                sp.wait_ge(y_added, 16 * NBUF * n)
                sp.dma_start(x[:, :, :], acc[0:T, :].rearrange("(t p) d -> p t d", p=P)).then_inc(acc_in, 16)
                sp.wait_ge(acc_in, 16)

            @block.gpsimd
            def _(pool):
                def gather(r, k):
                    i = NBUF * r + k
                    pool.wait_ge(tables, 1)
                    if not (isinstance(r, int) and r == 0):
                        pool.wait_ge(xg_made, i - NBUF + 1)
                    nc.gpsimd.tensor_copy(gcol[:, k:k + 1], idx_tab[:, column(r, k)]).then_inc(gcol_set, 1)
                    col_set = count(pool, i + 1)
                    pool.wait_ge(tables, 1)
                    pool.wait_ge(gcol_set, col_set)
                    pool.indirect_dma_start(out=xg[k], out_offset=None, in_=xrow,
                                            in_offset=bass.IndirectOffsetOnAxis(ap=gcol[:, k:k + 1], axis=0)
                                            ).then_inc(xg_loaded[k], 16)

                def scatter(r, k):
                    i = NBUF * r + k
                    pool.wait_ge(acc_out, 32)
                    pool.wait_ge(y_ready, i + 1)
                    if not (isinstance(i, int) and i == 0):
                        pool.wait_ge(y_added, 16 * i)
                    nc.gpsimd.tensor_copy(scol[:, k:k + 1], idx_tab[:, column(r, k)]).then_inc(scol_set, 1)
                    col_set = count(pool, i + 1)
                    pool.wait_ge(tables, 1)
                    pool.wait_ge(scol_set, col_set)
                    pool.indirect_dma_start(out=acc, out_offset=bass.IndirectOffsetOnAxis(ap=scol[:, k:k + 1], axis=0),
                                            in_=yrow[k], in_offset=None, compute_op=ALU.add).then_inc(y_added, 16)

                n = iterations(pool)
                for k in range(NBUF):
                    gather(0, k)
                for k in range(NBUF):
                    gather(1, k)
                    scatter(0, k)
                with pool.Fori(2, n) as r:
                    for k in range(NBUF):
                        gather(r, k)
                        scatter(r - 1, k)
                for k in range(NBUF):
                    scatter(n - 1, k)

            @block.tensor
            def _(pe):
                def after_first(r, k):
                    return not (isinstance(r, int) and r == 0 and k == 0)

                def rows_t(r, k):
                    pe.wait_ge(xg_loaded[k], 16 * (r + 1))
                    if after_first(r, k):
                        pe.wait_ge(xg_ready, NBUF * r + k)
                    for c in range(NC):
                        last = nc.tensor.transpose(PS[:, 4, c * P:(c + 1) * P], xg[k][:, c * P:(c + 1) * P], ident[:, :])
                    last.then_inc(xg_made, 1)

                def gate_up(r, k, gu):
                    i = NBUF * r + k
                    if gu == 0:
                        pe.wait_ge(xg_ready, i + 1)
                        pe.wait_ge(w_gu[k], 16 * (r + 1))
                    if after_first(r, k):
                        pe.wait_ge(h_ready if gu else silu_ready, i)
                    for c in range(NC):
                        last = nc.tensor.matmul(PS[:, gu, 0:I], xgT[k % 2][:, c, :], wgu[k][:, c, gu, :],
                                                start=(c == 0), stop=(c == NC - 1))
                    last.then_inc(u_made if gu else g_made, 1)

                def hidden_t(r, k):
                    i = NBUF * r + k
                    pe.wait_ge(h_ready, i + 1)
                    if after_first(r, k):
                        pe.wait_ge(ht_ready, i)
                    for j, (i0, w) in enumerate(IJ):
                        last = nc.tensor.transpose(PS[0:w, 2, j * P:(j + 1) * P], hid[:, i0:i0 + w], ident[:, :])
                    last.then_inc(ht_made, 1)

                def down(r, k):
                    i = NBUF * r + k
                    pe.wait_ge(ht_ready, i + 1)
                    pe.wait_ge(w_dn[k], 32 * (r + 1))
                    if after_first(r, k):
                        pe.wait_ge(y_ready, i)
                    for j, (i0, w) in enumerate(IJ):
                        last = nc.tensor.matmul(PS[:, 3, :], hT[0:w, j, :], wdn[k][0:w, j, :],
                                                start=(j == 0), stop=(j == 2))
                    last.then_inc(y_made, 1)

                def step(r, k, more=True):
                    before = tile_before(r, k) if after_first(r, k) else None
                    gate_up(r, k, 0)
                    if before is not None:
                        hidden_t(*before)
                    if more:
                        rows_t(*tile_after(r, k))
                    gate_up(r, k, 1)
                    if before is not None:
                        down(*before)

                n = iterations(pe)
                pe.wait_ge(tables, 1)
                rows_t(0, 0)
                for k in range(NBUF):
                    step(0, k)
                with pe.Fori(1, n - 1) as r:
                    for k in range(NBUF):
                        step(r, k)
                for k in range(NBUF):
                    step(n - 1, k, more=k < NBUF - 1)
                hidden_t(n - 1, NBUF - 1)
                down(n - 1, NBUF - 1)

            @block.scalar
            def _(act):
                def rows_copy(r, k):
                    act.wait_ge(xg_made, NBUF * r + k + 1)
                    nc.scalar.copy(xgT[k % 2].rearrange("p a b -> p (a b)"), PS[:, 4, :]).then_inc(xg_ready, 1)

                def silu(r, k):
                    i = NBUF * r + k
                    act.wait_ge(g_made, i + 1)
                    if not (isinstance(i, int) and i == 0):
                        act.wait_ge(h_ready, i)
                    nc.scalar.activation(act_g, PS[:, 0, 0:I], ACT.Silu).then_inc(silu_ready, 1)

                def rows_out_copy(r, k):
                    i = NBUF * r + k
                    if isinstance(i, int) and i == 0:
                        act.wait_ge(acc_out, 32)
                    act.wait_ge(y_made, i + 1)
                    if not (isinstance(r, int) and r == 0):
                        act.wait_ge(y_added, 16 * (i - NBUF + 1))
                    nc.scalar.activation(yrow[k], PS[:, 3, :], ACT.Copy, scale=w_tab[:, column(r, k)]).then_inc(y_ready, 1)

                def step(r, k, more=True):
                    silu(r, k)
                    if more:
                        rows_copy(*tile_after(r, k))
                    if not (isinstance(r, int) and r == 0 and k == 0):
                        rows_out_copy(*tile_before(r, k))

                n = iterations(act)
                act.wait_ge(tables, 1)
                rows_copy(0, 0)
                for r in range(2):
                    for k in range(NBUF):
                        step(r, k)
                with act.Fori(2, n - 1) as r:
                    for k in range(NBUF):
                        step(r, k)
                for k in range(NBUF):
                    step(n - 1, k, more=k < NBUF - 1)
                rows_out_copy(n - 1, NBUF - 1)

            @block.vector
            def _(dve):
                def mul(r, k):
                    i = NBUF * r + k
                    dve.wait_ge(silu_ready, i + 1)
                    dve.wait_ge(u_made, i + 1)
                    if not (isinstance(i, int) and i == 0):
                        dve.wait_ge(ht_made, i)
                    nc.vector.tensor_tensor(hid, act_g, PS[:, 1, 0:I], ALU.mult).then_inc(h_ready, 1)

                def hidden_copy(r, k):
                    i = NBUF * r + k
                    dve.wait_ge(ht_made, i + 1)
                    if not (isinstance(i, int) and i == 0):
                        dve.wait_ge(y_made, i)
                    nc.vector.tensor_copy(hT[:, 0:2, :], PS[:, 2, 0:2 * P].rearrange("p (a b) -> p a b", a=2))
                    nc.vector.tensor_copy(hT[0:96, 2, :], PS[0:96, 2, 2 * P:3 * P]).then_inc(ht_ready, 1)

                n = iterations(dve)
                dve.wait_ge(tables, 1)
                for k in range(NBUF):
                    if k:
                        hidden_copy(0, k - 1)
                    mul(0, k)
                with dve.Fori(1, n) as r:
                    for k in range(NBUF):
                        hidden_copy(*tile_before(r, k))
                        mul(r, k)
                hidden_copy(n - 1, NBUF - 1)


        GROUPS = []
        for c in range(4):
            GROUPS += [("k", 0, c), ("k", 1, c)]
            GROUPS += [("v", kt, c) for kt in range(KT_N) if kt // 4 == c]
        NGR = len(GROUPS)
        NK = [sum(1 for q in GROUPS[:g] if q[0] == "k") for g in range(NGR + 1)]
        NV = [sum(1 for q in GROUPS[:g] if q[0] == "v") for g in range(NGR + 1)]
        SHARE = [([0, 1, 2], [3], [4], [5]), ([6, 7], [8], [9], [10]),
                 ([11, 12], [13], [14], [15]), ([16, 17], [18], [19], [20])]
        HIGH_AT = [(0, 1), (0, 2), (0, 3), (1, 0)]
        KTS = [[kt for kt in range(KT_N) if kt // 4 == tg] for tg in range(4)]
        rows = lambda kt: min(P, S2 - kt * P)
        half_of = lambda hf, g: 6 + (NGR * hf + g) % 2

        with nc.Block() as block:
            @block.sync
            def _(sp):
                sp.dma_start(wq1, a["l1_wq"]).then_inc(ld_l1q, 16)
                sp.dma_start(bias_r[:, :], a["l1_bo"].to_broadcast([P, D])).then_inc(ld_bo1, 16)

                def load_ctx(b, bv):
                    for c, (k0, n) in enumerate(KC):
                        sp.wait_ge(vx_made, KT_N * (2 * b - 1) + sum(len(q) for q in KTS[:c + 1]))
                        sp.dma_start(ctx_raw[c][:, :, 0:n],
                                     a["ctxT"][bv, :, :, k0:k0 + n].rearrange("e p c k -> (e p) c k")
                                     ).then_inc(ctx_ld[c], 16)

                sp.wait_ge(mask_set, 1)
                sp.dma_start(mask8[:, :], a["mask"][1:2, :].to_broadcast([P, S2])).then_inc(mask_ld, 16)
                load_ctx(1, slice(1, 2))
                with sp.Fori(2, B) as b:
                    sp.wait_ge(ld_l1q, 16)
                    sp.wait_ge(mask_set, b)
                    sp.dma_start(mask8[:, :], a["mask"][bass.ds(b, 1), :].to_broadcast([P, S2])).then_inc(mask_ld, 16)
                    load_ctx(b, bass.ds(b, 1))
                sp.wait_ge(vx_made, KT_N * 2 * B)
                sp.dma_start(slot[2][:, :, :], a["l1_wo"]).then_inc(ld_l1o, 16)
                sp.dma_start(slot[3][:, :, :], a["l1a_wq"]).then_inc(ld_l1a, 16)
                sp.dma_start(slot[0][:, :, :], a["l1a_wk"]).then_inc(ld_l1a, 16)
                sp.dma_start(slot[1][:, :, :], a["l1a_wv"]).then_inc(ld_l1a, 16)
                sp.wait_ge(xb_ready, 3)
                sp.wait_ge(xx_ready, NT)
                sp.dma_start(bias_r[:, :], a["l1a_bo"].to_broadcast([P, D])).then_inc(ld_boa1, 16)
                sp.dma_start(slot[2][:, :, :], a["l1a_wo"]).then_inc(ld_l1ao, 16)

            @block.gpsimd
            def _(pool):
                for v in (ctx_hi, ctx_lo):
                    pad = v[3][:, :, KC[3][1]:]
                    nc.gpsimd.tensor_copy(pad, ident[:, KC[3][1]:].unsqueeze(1).to_broadcast([P, NC, P - KC[3][1]])
                                          ).then_inc(pads_set, 1)
                ln_pool(pool, 3)

                def rest(lo, raw, hi, s, sem_in, n):
                    pool.wait_ge(sem_in, n)
                    nc.gpsimd.tensor_tensor(lo, raw, hi.bitcast(F32), ALU.subtract).then_inc(s, 1)

                def ctx_rest(b, c):
                    k = KC[c][1]
                    rest(ctx_lo[c][:, :, 0:k], ctx_raw[c][:, :, 0:k], ctx_hi[c][:, :, 0:k], lo_ready,
                         hi_ready, 4 * b + c + 1)

                rest(wkv_lo[0], slot[1], wkv_hi[0], w_lo, w_hi, 1)
                ctx_rest(0, 0)
                rest(wkv_lo[1], slot[3], wkv_hi[1], w_lo, w_hi, 2)
                for c in range(1, 4):
                    ctx_rest(0, c)

                def take_q(b, hf, bv):
                    nc.gpsimd.tensor_copy(qbh[hf][:, :, :].unsqueeze(2), qbd[:, 2 * hf:2 * hf + 2, bv, :]
                                          ).then_inc(qh_ready, 1)

                pool.wait_ge(q_ready, 3 * NC)
                take_q(0, 0, slice(0, 1))
                take_q(0, 1, slice(0, 1))
                pool.wait_ge(ld_bo1, 16)
                add_out_bias(pool, 2, 4)
                with pool.Fori(1, B) as b:
                    for hf in range(2):
                        for c in ((0, 1, 2), (3,))[hf]:
                            ctx_rest(b, c)
                        pool.wait_ge(q_ready, 3 * NC)
                        pool.wait_ge(sx_made, 32 * b + 16 * hf - 16)
                        take_q(b, hf, bass.ds(b, 1))

            @block.tensor
            def _(pe):
                def group(b, hf, g):
                    kind, i, c = GROUPS[g]
                    u = 2 * b + hf
                    bank = half_of(hf, g)
                    if hf == 0 and (g == 0 or GROUPS[g - 1][2] != c):
                        pe.wait_ge(lo_ready, 4 * b + c + 1)
                    if g >= 2 or not (isinstance(b, int) and b == 0 and hf == 0):
                        g2, u2 = (g - 2, u) if g >= 2 else (NGR + g - 2, u - 1)
                        if GROUPS[g2][0] == "k":
                            pe.wait_ge(kx_ready, 8 * u2 + NK[g2 + 1])
                        else:
                            pe.wait_ge(vx_ready, KT_N * u2 + NV[g2 + 1])
                    if kind == "k":
                        k0, n = KC[c]
                        f0 = (2 * hf + i) * P
                        n += n % 2
                        for cc in range(NC):
                            for w, x3 in ((wkv_hi, ctx_hi), (wkv_lo, ctx_hi), (wkv_hi, ctx_lo)):
                                last = nc.tensor.matmul(PS[:, bank, 0:n], w[0][:, cc, f0:f0 + P], x3[c][:, cc, 0:n],
                                                        start=(cc == 0 and w is wkv_hi and x3 is ctx_hi),
                                                        stop=(cc == NC - 1 and x3 is ctx_lo))
                        last.then_inc(kx_made, 1)
                    else:
                        f0, k0 = hf * 256, i % 4 * P
                        for cc in range(NC):
                            for w, x3 in ((wkv_hi, ctx_hi), (wkv_hi, ctx_lo), (wkv_lo, ctx_hi)):
                                last = nc.tensor.matmul(PS[:, bank, 0:256], x3[c][:, cc, k0:k0 + P],
                                                        w[1][:, cc, f0:f0 + 256],
                                                        start=(cc == 0 and w is wkv_hi and x3 is ctx_hi),
                                                        stop=(cc == NC - 1 and w is wkv_lo))
                        last.then_inc(vx_made, 1)

                def score(b, hf, j, c):
                    u, r, (k0, n) = 2 * b + hf, 64 * (j % 2), KC[c]
                    if j == 0 and c == 0:
                        pe.wait_ge(qh_ready, u + 1)
                        pe.wait_ge(kx_ready, 8 * (u + 1))
                    if c >= 2:
                        pe.wait_ge(sx_read, 16 * u + 4 * j + c - 1)
                    nc.tensor.matmul(PS[:, c % 2, 0:n], qbh[hf][r:r + 64, j // 2, :],
                                     kTx[hf][r:r + 64, j // 2, k0:k0 + n], start=True, stop=True).then_inc(sx_made, 1)

                def turn_p(u, j, tg):
                    if tg == 0:
                        pe.wait_ge(px_ready, 4 * u + j + 1)
                    for i, kt in enumerate(KTS[tg]):
                        n = rows(kt)
                        last = nc.tensor.transpose(PS[0:n, 2 + tg % 2, i * P:(i + 1) * P],
                                                   sx[j % 2][:, kt * P:kt * P + n], ident[:, :])
                    last.then_inc(ptx_made, 1)

                def pv(u, hf, j, tg):
                    pe.wait_ge(ptx_dve if tg % 2 else ptx_act, 8 * u + 2 * j + tg // 2 + 1)
                    if tg == 0:
                        pe.wait_ge(zx_ready, 4 * u + j + 1)
                        if j == 0:
                            pe.wait_ge(vx_ready, KT_N * (u + 1))
                    for i, kt in enumerate(KTS[tg]):
                        n = rows(kt)
                        last = nc.tensor.matmul(PS[:, 4, 0:64], pTx[tg % 2][0:n, i, :],
                                                vx[hf][0:n, kt, j * 64:(j + 1) * 64],
                                                start=(kt == 0), stop=(kt == KT_N - 1))
                    last.then_inc(pvx_part, 1)

                def project(t):
                    if t < 2:
                        pe.wait_ge(vx_ready, KT_N * 2 * B)
                        pe.wait_ge(kx_ready, 8 * 2 * B)
                        pe.wait_ge(ld_l1o, 16)
                    else:
                        pe.wait_ge(xx_ready, t - 1)
                    for jh in range(4):
                        last = nc.tensor.matmul(PS[:, 6 + t % 2, :], zT[:, jh // 2, jh % 2, t * P:(t + 1) * P],
                                                slot[2][:, jh, :], start=(jh == 0), stop=(jh == 3))
                    last.then_inc(pj1_made, 1)

                def unit(b, hf, nxt):
                    u = 2 * b + hf
                    for j in range(4):
                        share = SHARE[j] if nxt is not None else ([], [], [], [])
                        for g in share[0]:
                            group(*nxt, g)
                        turn_p(u, j, 0)
                        turn_p(u, j, 1)
                        for g in share[1]:
                            group(*nxt, g)
                        if nxt is None and j < NT - 1:
                            project(j)
                        pv(u, hf, j, 0)
                        pv(u, hf, j, 1)
                        turn_p(u, j, 2)
                        turn_p(u, j, 3)
                        for g in share[2]:
                            group(*nxt, g)
                        pv(u, hf, j, 2)
                        pv(u, hf, j, 3)
                        ahead = (b, hf, j + 1) if j < 3 else (None if nxt is None else (*nxt, 0))
                        if ahead:
                            score(*ahead, 0)
                            score(*ahead, 1)
                        if j == 3:
                            pe.wait_ge(zx_ready, 4 * u + 5)
                            pe.wait_ge(ztx_ready, u + 1)
                            nc.tensor.transpose(PS[:, 5, 0:P], z[:, hf, 0:4, :].rearrange("p a b -> p (a b)"),
                                                ident[:, :]).then_inc(ztx_made, 1)
                        for g in share[3]:
                            group(*nxt, g)
                        if ahead:
                            score(*ahead, 2)
                            score(*ahead, 3)

                xt_pe(pe, 3)
                pe.wait_ge(ld_l1q, 16)
                q_pe(pe, wq1, 3, 2)
                pe.wait_ge(q_ready, 3 * NC)
                pe.wait_ge(w_lo, 2)
                pe.wait_ge(pads_set, 2)
                for g in range(NGR):
                    group(0, 0, g)
                for c in range(4):
                    score(0, 0, 0, c)
                with pe.Fori(0, B - 1) as b:
                    unit(b, 0, (b, 1))
                    unit(b, 1, (b + 1, 0))
                unit(B - 1, 0, (B - 1, 1))
                unit(B - 1, 1, None)
                pe.wait_ge(ztx_ready, 2 * B + 1)
                project(NT - 1)

            @block.scalar
            def _(act):
                def k_out(b, hf, g):
                    kind, i, c = GROUPS[g]
                    if kind == "k":
                        k0, n = KC[c]
                        act.wait_ge(kx_made, 8 * (2 * b + hf) + NK[g + 1])
                        nc.scalar.activation(kTx[hf][:, i, k0:k0 + n], PS[:, half_of(hf, g), 0:n], ACT.Identity,
                                             bias=bias_c[:, 3, 2 * hf + i:2 * hf + i + 1]).then_inc(kx_ready, 1)

                def ex(u, j):
                    act.wait_ge(sx_max, 4 * u + j + 1)
                    nc.scalar.activation(sx[j % 2][:, 0:S2], sx[j % 2][:, 0:S2], ACT.Exp, scale=SC,
                                         bias=nmx[:, j % 2:j % 2 + 1],
                                         accum_out=rsx[:, j % 2:j % 2 + 1]).then_inc(px_ready, 1)

                def ctx_high(b, c):
                    act.wait_ge(ctx_ld[c], 16 * (b + 1))
                    k = KC[c][1]
                    nc.scalar.copy(ctx_hi[c][:, :, 0:k], ctx_raw[c][:, :, 0:k]).then_inc(hi_ready, 1)

                def unit(b, hf, nxt, bv):
                    u = 2 * b + hf
                    more = not isinstance(b, int)
                    for j in range(4):
                        share = SHARE[j] if nxt is not None else ([], [], [], [])
                        for g in share[0]:
                            k_out(*nxt, g)
                        for tg in (0, 2):
                            act.wait_ge(ptx_made, 16 * u + 4 * j + tg + 1)
                            nc.scalar.copy(pTx[0][:, :, :].rearrange("p a b -> p (a b)"),
                                           PS[:, 2, :]).then_inc(ptx_act, 1)
                            for g in share[1 + tg // 2]:
                                k_out(*nxt, g)
                        if j == 3:
                            act.wait_ge(ztx_made, u + 1)
                            nc.scalar.copy(zT[:, hf, :, bv],
                                           PS[:, 5, 0:P].rearrange("p (h q) -> p h q", h=2)).then_inc(ztx_ready, 1)
                        for g in share[3]:
                            k_out(*nxt, g)
                        if j < 3:
                            ex(u, j + 1)
                        elif nxt is not None:
                            ex(u + 1, 0)
                        if more and (hf, j) in HIGH_AT:
                            ctx_high(b + 1, HIGH_AT.index((hf, j)))

                nc.scalar.copy(rsx[:, :], ident[:, 0:2]).then_inc(ztx_ready, 1)
                act.wait_ge(ld_wkv, 32)
                for i in range(2):
                    nc.scalar.copy(wkv_hi[i], slot[1 + 2 * i][:, :, :]).then_inc(w_hi, 1)
                ctx_high(0, 0)
                xt_copy(act, nc.scalar.copy, 3, (0, 2))
                ctx_high(0, 1)
                act.wait_ge(xt_made, NT * 4)
                ctx_high(0, 2)
                ctx_high(0, 3)
                for g in range(NGR):
                    k_out(0, 0, g)
                ex(0, 0)
                with act.Fori(0, B - 1) as b:
                    unit(b, 0, (b, 1), bass.ds(S1 * b, S1))
                    unit(b, 1, (b + 1, 0), bass.ds(S1 * b, S1))
                unit(B - 1, 0, (B - 1, 1), slice(T - S1, T))
                unit(B - 1, 1, None, slice(T - S1, T))

            @block.vector
            def _(dve):
                link = Chain(dve, dve_seq3)
                seq = dve_x

                def v_out(b, hf, g):
                    kind, i, c = GROUPS[g]
                    if kind == "v":
                        n = rows(i)
                        dve.wait_ge(vx_made, KT_N * (2 * b + hf) + NV[g + 1])
                        nc.vector.tensor_tensor(vx[hf][0:n, i, :], PS[0:n, half_of(hf, g), 0:256],
                                                vbias[0:n, hf * 256:hf * 256 + 256], ALU.add).then_inc(vx_ready, 1)

                def masked(u, j, c):
                    k0, n = KC[c]
                    made = count(dve, 16 * u + 4 * j + c + 1)
                    dve.wait_ge(ld_vb1, 16)
                    dve.wait_ge(sx_made, made)
                    nc.vector.tensor_tensor_reduce(out=sx[j % 2][:, k0:k0 + n], in0=PS[:, c % 2, 0:n],
                                                   in1=maskadd[:, k0:k0 + n], scale=1.0, scalar=-3e38, op0=ALU.add,
                                                   op1=ALU.max, accum_out=mx4[:, c:c + 1]).then_inc(sx_read, 1)

                def row_max(u, j):
                    n = 4 * u + j
                    dve.wait_ge(sx_read, 4 * n + 4)
                    nc.vector.tensor_reduce(nmx[:, j % 2:j % 2 + 1], mx4[:, :], AX.X, ALU.max).then_inc(seq, 1)
                    dve.wait_ge(seq, n + 1)
                    nc.vector.tensor_scalar(nmx[:, j % 2:j % 2 + 1], nmx[:, j % 2:j % 2 + 1], -SC, None,
                                            ALU.mult).then_inc(sx_max, 1)

                def set_mask(count):
                    dve.wait_ge(mask_ld, 16 * count)
                    nc.vector.tensor_scalar(maskadd[:, :], mask8[:, :], NEG, None, ALU.mult).then_inc(mask_set, 1)
                    dve.wait_ge(mask_set, count)

                def project_out(t):
                    dve.wait_ge(xb_ready, 3)
                    dve.wait_ge(pj1_made, t + 1)
                    nc.vector.tensor_tensor(x[:, t, :], x[:, t, :], PS[:, 6 + t % 2, :], ALU.add).then_inc(xx_ready, 1)

                def unit(b, hf, nxt):
                    u = 2 * b + hf
                    for j in range(4):
                        share = SHARE[j] if nxt is not None else ([], [], [], [])
                        for g in share[0]:
                            v_out(*nxt, g)
                        dve.wait_ge(px_ready, 4 * u + j + 1)
                        nc.vector.reciprocal(rix[:, j % 2:j % 2 + 1], rsx[:, j % 2:j % 2 + 1]).then_inc(rix_ready, 1)
                        for tg in (1, 3):
                            dve.wait_ge(ptx_made, 16 * u + 4 * j + tg + 1)
                            n = rows(KTS[tg][0]) if tg == 3 else P
                            w = len(KTS[tg]) * P
                            nc.vector.tensor_copy(pTx[1][0:n, :, :].rearrange("p a b -> p (a b)")[:, 0:w],
                                                  PS[0:n, 3, 0:w]).then_inc(ptx_dve, 1)
                            for g in share[1 + tg // 2]:
                                v_out(*nxt, g)
                            if nxt is None and tg == 1 and j < NT - 1:
                                project_out(j)
                        dve.wait_ge(rix_ready, 4 * u + j + 1)
                        dve.wait_ge(pvx_part, 16 * u + 4 * j + 4)
                        for h in range(2):
                            r = slice(64 * h, 64 * h + 64)
                            ins = nc.vector.tensor_scalar(z[r, hf, j, :], PS[r, 4, h * HD:(h + 1) * HD],
                                                          rix[r, j % 2:j % 2 + 1], None, ALU.mult)
                        ins.then_inc(zx_ready, 1)
                        if hf == 1 and j == 3 and nxt is not None:
                            set_mask(b + 2)
                        ahead = (u, j + 1) if j < 3 else (None if nxt is None else (u + 1, 0))
                        if ahead:
                            masked(*ahead, 0)
                            masked(*ahead, 1)
                        for g in share[3]:
                            v_out(*nxt, g)
                        if ahead:
                            masked(*ahead, 2)
                            masked(*ahead, 3)
                            row_max(*ahead)

                nc.vector.memset(rix[:, :], 0.0).then_inc(zx_ready, 1)
                ln_dve(dve, link, 3)
                xt_copy(dve, nc.vector.tensor_copy, 3, (1, 3))
                q_dve(dve, 2, 2)
                set_mask(1)
                dve.wait_ge(ld_vb1, 16)
                for g in range(NGR):
                    v_out(0, 0, g)
                for c in range(4):
                    masked(0, 0, c)
                row_max(0, 0)
                with dve.Fori(0, B - 1) as b:
                    unit(b, 0, (b, 1))
                    unit(b, 1, (b + 1, 0))
                unit(B - 1, 0, (B - 1, 1))
                unit(B - 1, 1, None)
                project_out(NT - 1)
                dve.wait_ge(xx_ready, NT)

        with nc.Block() as block:
            @block.sync
            def _(sp):
                sp.dma_start(rhs, a["l1_rhs"]).then_inc(ld_rhs, 16)
                for t in range(NT):
                    sp.wait_ge(ff_x, t + 1)
                    sp.dma_start(out[t * P:(t + 1) * P, :], x[:, t, :]).then_inc(out_done, 16)
                sp.wait_ge(out_done, 16 * NT)

            @block.gpsimd
            def _(pool):
                link = Chain(pool, pool_seq4)
                ln_pool(pool, 4)
                pool.wait_ge(ld_boa1, 16)
                add_out_bias(pool, 3, 5)
                pool.wait_ge(rabs_ready, 1)
                nc.gpsimd.partition_all_reduce(rscale, rabs, P, RMAX).then_inc(rmax_ready, 1)
                ln_pool(pool, 5)

            @block.tensor
            def _(pe):
                xt_pe(pe, 4)
                pe.wait_ge(ld_l1a, 48)
                q_pe(pe, slot[3], 4, 3)
                for dc in range(NC):
                    for c in range(NC):
                        last = nc.tensor.matmul(PS[:, dc, :], slot[0][:, c, dc * P:(dc + 1) * P], xnT[:, c, :],
                                                start=(c == 0), stop=(c == NC - 1))
                    last.then_inc(k_made, 1)
                pe.wait_ge(q_ready, 4 * NC)
                for t in range(NT):
                    for c in range(NC):
                        last = nc.tensor.matmul(PS[:, 4 + t, :], xnT[:, c, t * P:(t + 1) * P], slot[1][:, c, :],
                                                start=(c == 0), stop=(c == NC - 1))
                    last.then_inc(v_made, 1)
                pe.wait_ge(k_ready, 3 * NC)
                pe.wait_ge(v_ready, 3 * NT)
                pe.wait_ge(ld_l1ao, 16)
                att_pe(pe, 2, slot[2])
                for t in range(NT):
                    pe.wait_ge(lq_made, t + 1)
                    for c in range(NC):
                        last = nc.tensor.transpose(PS[:, t, c * P:(c + 1) * P], xn[:, t, c * P:(c + 1) * P], ident[:, :])
                    last.then_inc(xt_made, 1)
                pe.wait_ge(rq_ready, 1)
                for t in range(NT):
                    pe.wait_ge(lq_ready, t + 1)
                    for c in range(NC):
                        last = nc.tensor.matmul(PS[:, 4 + t, :], lq[:, c, t * P:(t + 1) * P], rq[:, c, :],
                                                start=(c == 0), stop=(c == NC - 1))
                    last.then_inc(ff_made, 1)

            @block.scalar
            def _(act):
                xt_copy(act, nc.scalar.copy, 4, (0, 2))
                for dc in range(NC):
                    act.wait_ge(k_made, NC + dc + 1)
                    nc.scalar.copy(kT[:, dc, :], PS[:, dc, :]).then_inc(k_ready, 1)
                for t in range(NT):
                    act.wait_ge(v_made, 2 * NT + t + 1)
                    nc.scalar.copy(v64[:, t, :], PS[:, 4 + t, :]).then_inc(v_ready, 1)
                att_act(act, 2, SC)
                for t in range(NT):
                    act.wait_ge(xt_made, 5 * NT + t + 1)
                    nc.scalar.copy(lq[:, :, t * P:(t + 1) * P],
                                   PS[:, t, :].rearrange("p (c k) -> p c k", c=NC)).then_inc(lq_ready, 1)

            @block.vector
            def _(dve):
                link = Chain(dve, dve_seq4)
                ln_dve(dve, link, 4)
                xt_copy(dve, nc.vector.tensor_copy, 4, (1, 3))
                q_dve(dve, 3, None)
                dve.wait_ge(ld_rhs, 16)
                nc.vector.tensor_reduce(rabs, rhs.rearrange("p c d -> p d c"), AX.X, ALU.max,
                                        apply_absolute_value=True).then_inc(rabs_ready, 1)

                def rhs_scale():
                    dve.wait_ge(rmax_ready, 1)
                    link(nc.vector.tensor_scalar(rscale, rscale, 1e-12, 1.0 / 127.0, ALU.max, ALU.mult))
                    link(nc.vector.reciprocal(rabs, rscale))

                def rhs_rounded():
                    link(nc.vector.tensor_tensor(rtmp, rhs, rabs.unsqueeze(1).to_broadcast([P, NC, D]), ALU.mult))
                    link(nc.vector.tensor_scalar(rtmp, rtmp, ROUND, None, ALU.add))

                def rhs_integers():
                    nc.vector.tensor_scalar(rq, rtmp, -ROUND, None, ALU.add).then_inc(rq_ready, 1)

                att_dve(dve, link, 2, True, (rhs_scale, rhs_rounded, rhs_integers))
                ln_dve(dve, link, 5)
                dve.wait_ge(xn_ready, 6 * NT)
                link(nc.vector.tensor_reduce(lscale, xn[:, :, :], AX.X, ALU.max, apply_absolute_value=True))
                link(nc.vector.tensor_scalar(lscale, lscale, 1e-12, 1.0 / 127.0, ALU.max, ALU.mult))
                link(nc.vector.reciprocal(linv, lscale))
                for t in range(NT):
                    last = nc.vector.tensor_scalar(xn[:, t, :], xn[:, t, :], linv[:, t:t + 1], ROUND,
                                                   ALU.mult, ALU.add)
                link(last)
                for t in range(NT):
                    nc.vector.tensor_scalar(xn[:, t, :], xn[:, t, :], -ROUND, None, ALU.add).then_inc(lq_made, 1)
                for t in range(NT):
                    dve.wait_ge(ff_made, t + 1)
                    nc.vector.scalar_tensor_tensor(out=rtmp[:, t, :], in0=PS[:, 4 + t, :], scalar=lscale[:, t:t + 1],
                                                   in1=rscale, op0=ALU.mult, op1=ALU.mult).then_inc(ff_y, 1)
                    dve.wait_ge(ff_y, t + 1)
                    nc.vector.tensor_tensor(x[:, t, :], x[:, t, :], rtmp[:, t, :], ALU.add).then_inc(ff_x, 1)


def _lin(w):
    return w.reshape(-1, P, w.shape[1]).transpose(1, 0, 2)


def _heads(w):
    return w.reshape(2, 4, 2, HD, w.shape[1]).transpose(1, 3, 0, 2, 4).reshape(P, 4, w.shape[1])


def _heads64(w):
    return w.reshape(4, 2, 2, HD, w.shape[1]).transpose(0, 3, 1, 2, 4).reshape(P, 4, w.shape[1])


def kernel(**inputs):
    import numpy as _np
    import concourse.bacc as _bacc
    from concourse.bass_utils import run_bass_kernel_spmd as _run

    g = {k: _np.asarray(v) for k, v in inputs.items()}
    col = lambda b: b.reshape(NC, P).T
    row = lambda b: b.reshape(1, -1)
    ctxT = g["ctx_1024"].transpose(0, 2, 1)
    gate = _np.concatenate([g["L0_ffn_Wg"], g["L0_ffn_Sg"].reshape(2, I, D)])
    up = _np.concatenate([g["L0_ffn_Wu"], g["L0_ffn_Su"].reshape(2, I, D)])
    down = _np.concatenate([g["L0_ffn_Wd"], g["L0_ffn_Sd"].reshape(D, 2, I).transpose(1, 0, 2)]).transpose(0, 2, 1)
    gu = _np.stack([gate, up], axis=1).reshape(NE, 2, I, NC, P).transpose(0, 4, 3, 1, 2)
    laid = {
        "x": g["x"].reshape(NT, P, D).transpose(1, 0, 2),
        "ctx0": ctxT[:, :, :S1].reshape(B, NC, P, S1).transpose(2, 1, 0, 3).reshape(P, NC, T),
        "ctxT": ctxT.reshape(B, NC, P, S2).transpose(0, 2, 1, 3),
        "mask": g["mask_BxS2_bk0"],
        "l0_wq": _lin(g["L0_xattn_wq"]), "l0_wk": _lin(g["L0_xattn_wk"]), "l0_wv": _lin(g["L0_xattn_wv"]),
        "l0_wo": _heads64(g["L0_xattn_wo"]),
        "l0_bv": row(g["L0_xattn_bv"]), "l0_bo": row(g["L0_xattn_bo"]),
        "bias_c": _np.stack([col(g["L0_xattn_bq"]), col(g["L0_xattn_bk"]), col(g["L1_xattn_bq"]),
                             col(g["L1_xattn_bkv"][:D])], axis=1),
        "l0a_wq": g["L0_attn_Wq"].reshape(NC, 4, HD, HD).transpose(1, 3, 0, 2).reshape(P, NC, HD),
        "l0a_wp": _heads64(g["L0_attn_Wp"].T), "l0a_bp": row(g["L0_attn_bp"]),
        "gate_w": _lin(g["L0_ffn_gate_w"].T), "gate_b": row(g["L0_ffn_gate_bias"]),
        "w_gu2": gu.reshape(NE, P, NC * 2 * I),
        "w_dna2": down[:, :2 * P].reshape(NE, 2, P, D).transpose(0, 2, 1, 3).reshape(NE, P, 2 * D),
        "w_dnb": down[:, 2 * P:],
        "l1_wq": _lin(g["L1_xattn_Wq"]), "l1_wkv": _lin(g["L1_xattn_Wkv"]), "l1_bv": row(g["L1_xattn_bkv"][D:]),
        "l1_wo": _heads(g["L1_xattn_Wo"]), "l1_bo": row(g["L1_xattn_bo"]),
        "l1a_wq": _lin(g["L1_attn_Wq"].T), "l1a_wk": _lin(g["L1_attn_Wk"].T), "l1a_wv": _lin(g["L1_attn_Wv"].T),
        "l1a_wo": _heads64(g["L1_attn_Wo"].T), "l1a_bo": row(g["L1_attn_bo"]),
        "l1_rhs": _lin(g["L1_ffn_rhs"]),
    }
    nc = _bacc.Bacc("TRN2", target_bir_lowering=False, num_devices=1)
    arrays, args = {}, {}
    for name, v in laid.items():
        v = _np.ascontiguousarray(v)
        arrays[f"in_{name}"] = v
        args[name] = nc.dram_tensor(f"in_{name}", v.shape, mybir.dt.from_np(v.dtype), kind="ExternalInput").ap()
    args["w_gu"] = args["w_gu2"].rearrange("e p (c g i) -> e p c g i", c=NC, g=2)
    args["w_dna"] = args["w_dna2"].rearrange("e p (c n) -> e p c n", c=2)
    y = nc.dram_tensor("out_0", (T, D), F32, kind="ExternalOutput").ap()
    perceiver(nc, args, y)
    r = _run(nc, [arrays], core_ids=[0])
    return r.results[0]["out_0"].reshape(B, S1, D)
```
